# Optimizing a Trainium2 kernel written in Bass

```python
import numpy as np
import jax
import jax.numpy as jnp

def _softmax(x, axis=-1):
    return jax.nn.softmax(x, axis=axis)

def _gelu(x):
    return jax.nn.gelu(x, approximate=True)

def _silu(x):
    return jax.nn.silu(x)

def _sigmoid(x):
    return jax.nn.sigmoid(x)

def _layernorm(x, axis=-1, eps=1e-05):
    m = jnp.mean(x, axis=axis, keepdims=True)
    v = jnp.var(x, axis=axis, keepdims=True)
    return (x - m) / jnp.sqrt(v + eps)

def _scatter_add(tgt, idx, src, axis=0):
    return tgt.at[idx].add(src)

def _segment_sum(src, seg, n):
    return jax.ops.segment_sum(src, seg, n)
kernel_name = 'mk_seq_preln_d1_jaxref_r4_07a966'

def setup_inputs(seed: int=0):
    np.random.seed(seed)
    _w = jnp.asarray

    def _L0_attn_setup():
        import jax, jax.numpy as jnp
        import numpy as np
        DIM = 512
        HEADS = 16
        HEAD_DIM = DIM // HEADS
        RANK = 16
        ALPHA = 8.0
        SCALING = ALPHA / RANK
        SCALE = HEAD_DIM ** (-0.5)

        def lora_linear(x, W, b, Bm, Am):
            out = jnp.einsum('bld,od->blo', x, W) + b
            upd = jnp.einsum('blr,or->blo', jnp.einsum('bld,rd->blr', x, Bm), Am)
            return out + SCALING * upd

        def _split(t):
            B, L, D = t.shape
            return t.reshape(B, L, HEADS, HEAD_DIM).transpose(0, 2, 1, 3)
        key = jax.random.key(seed)
        ks = jax.random.split(key, 20)
        B, L = (4, 512)
        x = jax.random.normal(ks[0], (B, L, DIM), dtype=jnp.float32)
        s = 0.02
        inp = {'x': x}
        for i, name in enumerate(['q', 'k', 'v', 'o']):
            inp[f'W{name}'] = jax.random.normal(ks[1 + 4 * i], (DIM, DIM), jnp.float32) * s
            inp[f'b{name}'] = jax.random.normal(ks[2 + 4 * i], (DIM,), jnp.float32) * s
            inp[f'B{name}'] = jax.random.normal(ks[3 + 4 * i], (RANK, DIM), jnp.float32) * s
            inp[f'A{name}'] = jax.random.uniform(ks[4 + 4 * i], (DIM, RANK), jnp.float32, -0.1, 0.1)
        return inp
    _L0_attn_in = _L0_attn_setup()

    def _L0_ffn_setup():
        import jax, jax.numpy as jnp
        import numpy as np

        def _sparsify_2to4(h):
            B, S, I = h.shape
            g = h.reshape(B, S, I // 4, 4)
            a = jnp.abs(g)
            _, idx = jax.lax.top_k(a, 2)
            pos = jnp.arange(4)
            mask = (pos == idx[..., 0:1]) | (pos == idx[..., 1:2])
            return (g * mask.astype(g.dtype)).reshape(B, S, I)
        key = jax.random.key(seed)
        k1, k2, k3, k4 = jax.random.split(key, 4)
        B, S, H, I = (4, 512, 512, 2048)
        x = jax.random.normal(k1, (B, S, H), dtype=jnp.float32)
        w_gate = jax.random.normal(k2, (H, I), dtype=jnp.float32) / np.sqrt(H)
        w_up = jax.random.normal(k3, (H, I), dtype=jnp.float32) / np.sqrt(H)
        w_down = jax.random.normal(k4, (I, H), dtype=jnp.float32) / np.sqrt(I)
        return {'x': x, 'w_gate': w_gate, 'w_up': w_up, 'w_down': w_down}
    _L0_ffn_in = _L0_ffn_setup()
    _d = {'L0_attn_x': _L0_attn_in['x'], 'L0_attn_Wq': _L0_attn_in['Wq'], 'L0_attn_bq': _L0_attn_in['bq'], 'L0_attn_Bq': _L0_attn_in['Bq'], 'L0_attn_Aq': _L0_attn_in['Aq'], 'L0_attn_Wk': _L0_attn_in['Wk'], 'L0_attn_bk': _L0_attn_in['bk'], 'L0_attn_Bk': _L0_attn_in['Bk'], 'L0_attn_Ak': _L0_attn_in['Ak'], 'L0_attn_Wv': _L0_attn_in['Wv'], 'L0_attn_bv': _L0_attn_in['bv'], 'L0_attn_Bv': _L0_attn_in['Bv'], 'L0_attn_Av': _L0_attn_in['Av'], 'L0_attn_Wo': _L0_attn_in['Wo'], 'L0_attn_bo': _L0_attn_in['bo'], 'L0_attn_Bo': _L0_attn_in['Bo'], 'L0_attn_Ao': _L0_attn_in['Ao'], 'L0_ffn_w_gate': _L0_ffn_in['w_gate'], 'L0_ffn_w_up': _L0_ffn_in['w_up'], 'L0_ffn_w_down': _L0_ffn_in['w_down']}
    _x0 = _d['L0_attn_x']
    _d['L0_attn_x'] = jax.random.normal(jax.random.fold_in(jax.random.key(seed), 1), (4, 512, 512), dtype=_x0.dtype)
    del _x0
    return _d

def reference(L0_attn_x, L0_attn_Wq, L0_attn_bq, L0_attn_Bq, L0_attn_Aq, L0_attn_Wk, L0_attn_bk, L0_attn_Bk, L0_attn_Ak, L0_attn_Wv, L0_attn_bv, L0_attn_Bv, L0_attn_Av, L0_attn_Wo, L0_attn_bo, L0_attn_Bo, L0_attn_Ao, L0_ffn_w_gate, L0_ffn_w_up, L0_ffn_w_down):

    def _L0_attn_ref(x, Wq, bq, Bq, Aq, Wk, bk, Bk, Ak, Wv, bv, Bv, Av, Wo, bo, Bo, Ao):
        import jax, jax.numpy as jnp
        import numpy as np
        DIM = 512
        HEADS = 16
        HEAD_DIM = DIM // HEADS
        RANK = 16
        ALPHA = 8.0
        SCALING = ALPHA / RANK
        SCALE = HEAD_DIM ** (-0.5)

        def lora_linear(x, W, b, Bm, Am):
            out = jnp.einsum('bld,od->blo', x, W) + b
            upd = jnp.einsum('blr,or->blo', jnp.einsum('bld,rd->blr', x, Bm), Am)
            return out + SCALING * upd

        def _split(t):
            B, L, D = t.shape
            return t.reshape(B, L, HEADS, HEAD_DIM).transpose(0, 2, 1, 3)
        q = _split(lora_linear(x, Wq, bq, Bq, Aq))
        k = _split(lora_linear(x, Wk, bk, Bk, Ak))
        v = _split(lora_linear(x, Wv, bv, Bv, Av))
        scores = jnp.einsum('bhqd,bhkd->bhqk', q, k) * SCALE
        attn = jax.nn.softmax(scores, axis=-1)
        out = jnp.einsum('bhqk,bhkd->bhqd', attn, v)
        B, H, L, hd = out.shape
        out = out.transpose(0, 2, 1, 3).reshape(B, L, H * hd)
        return lora_linear(out, Wo, bo, Bo, Ao)

    def _L0_ffn_ref(x, w_gate, w_up, w_down):
        import jax, jax.numpy as jnp
        import numpy as np

        def _sparsify_2to4(h):
            B, S, I = h.shape
            g = h.reshape(B, S, I // 4, 4)
            a = jnp.abs(g)
            _, idx = jax.lax.top_k(a, 2)
            pos = jnp.arange(4)
            mask = (pos == idx[..., 0:1]) | (pos == idx[..., 1:2])
            return (g * mask.astype(g.dtype)).reshape(B, S, I)
        h = jax.nn.silu(jnp.einsum('bsh,hi->bsi', x, w_gate)) * jnp.einsum('bsh,hi->bsi', x, w_up)
        h_sparse = _sparsify_2to4(h)
        return jnp.einsum('bsi,ih->bsh', h_sparse, w_down)
    x = L0_attn_x
    x = x + _L0_attn_ref(_layernorm(x, axis=-1), L0_attn_Wq, L0_attn_bq, L0_attn_Bq, L0_attn_Aq, L0_attn_Wk, L0_attn_bk, L0_attn_Bk, L0_attn_Ak, L0_attn_Wv, L0_attn_bv, L0_attn_Bv, L0_attn_Av, L0_attn_Wo, L0_attn_bo, L0_attn_Bo, L0_attn_Ao)
    x = x + _L0_ffn_ref(_layernorm(x, axis=-1), L0_ffn_w_gate, L0_ffn_w_up, L0_ffn_w_down)
    return x

_drawn_inputs = setup_inputs


def setup_inputs(seed=0):
    import zlib

    import numpy as np

    out = dict(_drawn_inputs(seed))
    spreads = {}
    factors = {'L0_attn_Wq': 6.704,
     'L0_attn_bq': 8.0,
     'L0_attn_Bq': 8.0,
     'L0_attn_Aq': 8.0,
     'L0_attn_Wk': 6.641,
     'L0_attn_bk': 200.0,
     'L0_attn_Bk': 8.0,
     'L0_attn_Ak': 8.0,
     'L0_attn_Wv': 3.156,
     'L0_attn_bv': 3.288,
     'L0_attn_Bv': 8.0,
     'L0_attn_Av': 8.0,
     'L0_attn_Bo': 8.0,
     'L0_attn_Ao': 8.0,
     'L0_attn_bo': 33.515}
    for name, (base, spread) in spreads.items():
        noise = np.random.default_rng([zlib.crc32(name.encode()), seed]).standard_normal(out[name].shape)
        drawn = base * np.exp(spread * noise) if base else spread * noise
        out[name] = jnp.asarray(drawn.astype(out[name].dtype))
    for name, factor in factors.items():
        out[name] = (out[name] * factor).astype(out[name].dtype)
    return out
```

```python
from contextlib import ExitStack

import concourse.bass as bass
import concourse.mybir as mybir

P = 128
F32 = mybir.dt.float32
F32R = mybir.dt.float32r
BF16 = mybir.dt.bfloat16
ALU = mybir.AluOpType
ACT = mybir.ActivationFunctionType
AX = mybir.AxisListType

BATCHES, L, D = 4, 512, 512
HEADS, HD, RANK = 16, 32, 16
FF = 2048
KT = D // P
TT = L // P
KK = L // P
GH = P // HD
GROUPS = HEADS // GH
NT = BATCHES * TT
J = 4
SB = FF // (J * P)
LORA = 8.0 / RANK
SCALE = HD ** -0.5
EPS = 1e-5
STACK = 3 * HD
UNITS = KK * GH
LAST = BATCHES - 1

PJ_LORA, PJ_LN, PJ_V, PJ_O = 4 * KT, TT, TT, TT
PJ_START = PJ_LORA + PJ_LN + 2 * 3 + PJ_V
AT_LN = 3 * KT
AT_QK = AT_LN + PJ_LN
AT_V = AT_QK + 2 * 3
AT_LORA_O = AT_V + PJ_V
PJ_BODY = 2 * GROUPS + PJ_LN + PJ_V + PJ_O
STACK_DMAS = 16 * 3 * GH

M_AFTER = [0, 0] + [1] * 12 + [2, 2]
LN_AFTER = {1: 1, 8: 2, 10: 3}


def pj_use(what, slot=0):
    if what in ("q", "k"):
        return (0, 6, 8, 10)[slot] + (what == "k")
    return {"ln": 2, "v": 12, "o": 16}[what]


def block_kernel(nc, x, wqkvo, lora_b, lora_a, bias_cols, bo_rows, w_gu, w_down, out):
    x2_dram = nc.dram_tensor("x2_dram", [NT, P, D], F32, kind="Internal").ap()
    x2_flat = x2_dram.rearrange("t p d -> (t p d)")
    x_rows = x.rearrange("p t d -> p (t d)")
    w_gu_rows = w_gu.rearrange("p s j a n -> p (s j a n)")
    w_down_rows = w_down.rearrange("p s j d -> p (s j d)")
    start = -(-nc.sbuf_base // 64) * 64

    with ExitStack() as ctx:
        def sb(name, at_kb, shape, dt=F32):
            return nc.alloc_sbuf_tensor_at(name, [P] + shape, dt, offset=start + int(at_kb * 1024))

        def sem(name):
            return ctx.enter_context(nc.semaphore(name))

        w_hi = [sb(f"w_hi_{n}", 16 * i, [KT, D], F32R) for i, n in enumerate("qkvo")]
        w_lo = [sb(f"w_lo_{n}", 16 * i + 8, [KT, D], F32R) for i, n in enumerate("qkvo")]
        w_raw = [sb(f"w_raw_{n}", 16 * i + 8, [KT, D]) for i, n in enumerate("qkvo")]
        xnT_hi = sb("xnT_hi", 64, [KT, L], F32R)
        xnT_lo = sb("xnT_lo", 72, [KT, L], F32R)
        qk_parts = sb("qk_parts", 80, [4, L], F32R)
        Q_HI, Q_LO, K_LO, K_HI = range(4)
        x_in = sb("x_in", 88, [2, D])
        x_res = sb("x_res", 92, [2, D])
        probs = sb("probs", 96, [2, GH, L])
        oT_hi = sb("oT_hi", 96, [GROUPS, L], F32R)
        oT_lo = sb("oT_lo", 104, [GROUPS, L], F32R)
        x_all = sb("x_all", 96, [NT, D])
        p_sum = sb("p_sum", 112, [GH, L])
        v_sb = sb("v_sb", 120, [KK, D])
        o_raw = sb("o_raw", 128, [GROUPS, L])
        recip = sb("recip", 136, [L])
        bo_sb = sb("bo_sb", 138, [D])
        stacks = [sb(f"stack{g}", 140 + 16 * g, [2, GH, L], F32R) for g in range(GROUPS)]
        lb_sb = sb("lb_sb", 188, [4, D])
        la_sb = sb("la_sb", 196, [4, D])
        ident = sb("ident", 204, [P])
        row_max = sb("row_max", 204.5, [P], F32R)
        stats = sb("stats", 205, [4, 6])
        mv = sb("mv", 205.25, [NT, 2])
        rstd = sb("rstd", 205.5, [NT])
        neg_half = sb("neg_half", 205.75, [NT])
        var_eps = sb("var_eps", 206, [NT])
        neg_max = sb("neg_max", 206.25, [2, UNITS])
        bias = sb("bias", 206.5, [3, KT])
        ones = sb("ones", 206.75, [HD])

        gu_hi = sb("gu_hi", 0, [J, 2, KT * P], F32R)
        gu_lo = sb("gu_lo", 16, [J, 2, KT * P], F32R)
        gu_raw = sb("gu_raw", 16, [J, 2, KT * P])
        dn_hi = sb("dn_hi", 32, [J, D], F32R)
        dn_lo = sb("dn_lo", 40, [J, D], F32R)
        dn_raw = sb("dn_raw", 40, [J, D])
        h = sb("h", 48, [J, L])
        h_abs = sb("h_abs", 56, [J, L])
        y = sb("y", 64, [NT, D])
        hT_hi = sb("hT_hi", 96, [J, L], F32R)
        hT_lo = sb("hT_lo", 104, [J, L], F32R)
        silu = sb("silu", 112, [2, L])
        pair_max = sb("pair_max", 116, [2, L])
        pair_min = sb("pair_min", 120, [2, L])
        first_wins = sb("first_wins", 124, [2, L], BF16)
        both_01 = sb("both_01", 126, [L], BF16)
        both_23 = sb("both_23", 127, [L], BF16)
        tilt = sb("tilt", 130, [L], BF16)
        wins_up = sb("wins_up", 126, [2, L], BF16)
        wins_down = sb("wins_down", 128, [2, L], BF16)
        xn2 = sb("xn2", 132, [TT, D])
        xn2T_hi = sb("xn2T_hi", 140, [KT, NT * P], F32R)
        xn2T_lo = sb("xn2T_lo", 172, [KT, NT * P], F32R)

        banks = [ctx.enter_context(nc.psum_tensor(f"bank{i}", [P, 512], F32)) for i in range(8)]
        ps_s, ps_m, ps_pj, ps_o, ps_sum = banks[0:2], banks[2:4], banks[4:6], banks[6], banks[7]
        ps_gate, ps_up, ps_y = banks[0:2], banks[2:4], banks[4:8]

        w_loaded = [sem(f"w_loaded_{n}") for n in "qkvo"]
        x_loaded = [sem(f"x_loaded{b}") for b in range(BATCHES)]
        lora_loaded, bias_loaded = sem("lora_loaded"), sem("bias_loaded")
        consts_ready, ident_zeroed = sem("consts_ready"), sem("ident_zeroed")
        stats_step, var_ready, rstd_ready = sem("stats_step"), sem("var_ready"), sem("rstd_ready")
        w_hi_done, w_lo_done = sem("w_hi_done"), sem("w_lo_done")
        x_in_loaded = [sem(f"x_in_loaded{i}") for i in range(2)]
        xn_ready = sem("xn_ready")
        pj_ready, pj_done = sem("pj_ready"), sem("pj_done")
        xnT_hi_done, qk_hi_done = sem("xnT_hi_done"), sem("qk_hi_done")
        stack_loaded = [sem(f"stack_loaded{g}") for g in range(GROUPS)]
        row_loaded = sem("row_loaded")
        m_ready, m_done = sem("m_ready"), sem("m_done")
        maxT_ready, maxT_done = sem("maxT_ready"), sem("maxT_done")
        s_ready, exp_done = sem("s_ready"), sem("exp_done")
        pv_done, psum_added = sem("pv_done"), sem("psum_added")
        sum_ready, recip_done, o_raw_done = sem("sum_ready"), sem("recip_done"), sem("o_raw_done")
        oT_hi_done, oT_lo_done = sem("oT_hi_done"), sem("oT_lo_done")
        x_res_loaded = [sem(f"x_res_loaded{i}") for i in range(2)]
        x_res_ready = sem("x_res_ready")
        x2_stored = [sem(f"x2_stored{i}") for i in range(2)]

        gu_loaded = [sem(f"gu_loaded{j}") for j in range(J)]
        dn_loaded = sem("dn_loaded")
        ffw_hi, ffw_lo = sem("ffw_hi"), sem("ffw_lo")
        x2_back = [sem(f"x2_back{c}") for c in range(BATCHES)]
        stats2_step, var2_ready, rstd2_ready = sem("stats2_step"), sem("var2_ready"), sem("rstd2_ready")
        xn2_ready, xn2T_ready = sem("xn2_ready"), sem("xn2T_ready")
        xn2T_hi_done, xn2T_done = sem("xn2T_hi_done"), sem("xn2T_done")
        gate_ready, up_ready = sem("gate_ready"), sem("up_ready")
        silu_done, h_ready, abs_done = sem("silu_done"), sem("h_ready"), sem("abs_done")
        mask_step, h_kept = sem("mask_step"), sem("h_kept")
        hT_hi_done, hT_lo_done = sem("hT_hi_done"), sem("hT_lo_done")
        down_ready, y_done = sem("down_ready"), sem("y_done")
        out_stored = sem("out_stored")

        def per_batch(body, eng, loop):
            body(0, True, False)
            with loop(1, LAST) as b:
                body(b, False, False)
            body(LAST, False, True)

        def per_block(step, loop):
            step(0, True, False)
            with loop(1, SB - 1) as s:
                step(s, False, False)
            step(SB - 1, False, True)

        def next_group(slot, b):
            return (slot + 1, b) if slot < GROUPS - 1 else (0, b + 1)

        def pj(b, what, slot=0, t=0):
            n = pj_use(what, slot)
            if isinstance(b, int) and b == LAST and what == "o":
                n = 2
            return PJ_START + PJ_BODY * b + n + t, (n + t) % 2

        block = ctx.enter_context(nc.Block())

        @block.sync
        def _(sp):
            sp.dma_start(x_all[:, 0:TT, :], x[:, 0:TT, :]).then_inc(x_loaded[0], 16)
            sp.dma_start(lb_sb[0:RANK], lora_b).then_inc(lora_loaded, 16)
            sp.dma_start(la_sb[0:RANK], lora_a).then_inc(lora_loaded, 16)
            for m in range(3):
                sp.dma_start(w_raw[m][:], wqkvo[m]).then_inc(w_loaded[m], 16)
                if m == 0:
                    sp.dma_start(bias[:], bias_cols).then_inc(bias_loaded, 16)
                    sp.dma_start(bo_sb[:], bo_rows).then_inc(bias_loaded, 16)
            for b in range(1, BATCHES):
                sp.dma_start(x_all[:, b * TT:(b + 1) * TT, :], x[:, b * TT:(b + 1) * TT, :]).then_inc(x_loaded[b], 16)
            sp.dma_start(w_raw[3][:], wqkvo[3]).then_inc(w_loaded[3], 16)

            def held(value):
                return value if isinstance(value, int) else sp.snap(value)

            def stack(g, split):
                sp.wait_ge(pj_done, split)
                for j in range(GH):
                    for row, (of_q, of_k) in enumerate(((Q_HI, K_HI), (Q_HI, K_LO), (Q_LO, K_HI))):
                        sp.dma_start(stacks[g][row * HD:(row + 1) * HD, :, j, :].bitcast(F32),
                                     qk_parts[j * HD:(j + 1) * HD, of_q:of_k + 1:of_k - of_q, :].bitcast(F32))\
                          .then_inc(stack_loaded[g], 16)

            for g in range(3):
                stack(g, AT_QK + 2 * g + 2)

            def body(b, first, last):
                for slot in range(GROUPS):
                    if not last and slot == 0:
                        for t in range(TT):
                            if t >= 2:
                                transposed = held(pj(b, "ln", 0, t - 2)[0] + 1)
                            else:
                                transposed = AT_QK if first else held(pj(b - 1, "ln", 0, t + 2)[0] + 1)
                            at = held(((b + 1) * TT + t) * D)
                            sp.wait_ge(pj_ready, transposed)
                            sp.dma_start(x_in[:, t % 2, :], x_rows[:, bass.ds(at, D)]).then_inc(x_in_loaded[t % 2], 16)
                    if slot == 0 or not last:
                        stack((slot + 3) % GROUPS, held(pj(b, "k", slot)[0] + 1))
                    if last and slot == 1:
                        sp.wait_ge(pj_ready, pj(b, "k", 0)[0] + 1)
                        for j in range(J):
                            sp.dma_start(gu_raw[:, j], w_gu[:, 0, j]).then_inc(gu_loaded[j], 16)
                        sp.dma_start(dn_raw[:], w_down[:, 0]).then_inc(dn_loaded, 16)
                        sp.wait_ge(stack_loaded[3], STACK_DMAS * BATCHES)
                        for c in range(BATCHES - 1):
                            if c == BATCHES - 2:
                                for i in range(2):
                                    sp.wait_ge(x2_stored[i], 16 * 2 * (BATCHES - 1))
                            sp.dma_start(y[:, c * TT:(c + 1) * TT, :],
                                         x2_dram[c * TT:(c + 1) * TT].rearrange("t p d -> p t d")).then_inc(x2_back[c], 16)
                for t in range(TT):
                    if t < 2:
                        at, stored = held((b * TT + t) * D), held(32 * b)
                        if not first:
                            sp.wait_ge(x2_stored[t], stored)
                        sp.dma_start(x_res[:, t, :], x_rows[:, bass.ds(at, D)]).then_inc(x_res_loaded[t], 16)
                for t in range(TT):
                    computed, at = held(pj(b, "o", 0, t)[0] + 1), held((b * TT + t) * P * D)
                    sp.wait_ge(pj_done, computed)
                    sp.dma_start(x2_flat[bass.ds(at, P * D)].rearrange("(p d) -> p d", p=P),
                                 x_res[:, t % 2, :]).then_inc(x2_stored[t % 2], 16)
                    if t < 2:
                        at, stored = held((b * TT + t + 2) * D), held(32 * b + 16)
                        sp.wait_ge(x2_stored[t], stored)
                        sp.dma_start(x_res[:, t, :], x_rows[:, bass.ds(at, D)]).then_inc(x_res_loaded[t], 16)

            per_batch(body, sp, sp.Fori)

            for i in range(2):
                sp.wait_ge(x2_stored[i], 32 * BATCHES)
            sp.dma_start(y[:, LAST * TT:, :], x2_dram[LAST * TT:].rearrange("t p d -> p t d")).then_inc(x2_back[LAST], 16)

            def block_step(s, first, last):
                if not first:
                    done, at = held(16 * s), held(s * J * D)
                    sp.wait_ge(down_ready, done)
                    sp.dma_start(dn_raw[:].rearrange("p j d -> p (j d)"), w_down_rows[:, bass.ds(at, J * D)]).then_inc(dn_loaded, 16)
                if not last:
                    for j in range(J):
                        done, at = held(16 * s + 12 + j + 1), held(((s + 1) * J + j) * 2 * KT * P)
                        sp.wait_ge(up_ready, done)
                        sp.dma_start(gu_raw[:, j].rearrange("p a n -> p (a n)"), w_gu_rows[:, bass.ds(at, 2 * KT * P)]).then_inc(gu_loaded[j], 16)

            per_block(block_step, sp.Fori)
            for c in range(BATCHES):
                sp.wait_ge(y_done, NT * (SB - 1) + TT * (c + 1))
                sp.dma_start(out[:, c * TT:(c + 1) * TT, :], y[:, c * TT:(c + 1) * TT, :]).then_inc(out_stored, 16)
            sp.wait_ge(out_stored, 16 * BATCHES)

        @block.tensor
        def _(pe):
            def three(dst, a_hi, a_lo, b_hi, b_lo, first, last):
                nc.tensor.matmul(dst, a_hi, b_hi, start=first, stop=False)
                nc.tensor.matmul(dst, a_hi, b_lo, start=False, stop=False)
                return nc.tensor.matmul(dst, a_lo, b_hi, start=False, stop=last)

            def pj_free(use):
                pe.wait_ge(pj_done, use - 1)

            def project_q(m, g, use, bank, tiles=range(KT)):
                if 0 in tiles:
                    pj_free(use)
                for c in tiles:
                    last = three(ps_pj[bank][:], w_hi[m][:, c, g * P:(g + 1) * P], w_lo[m][:, c, g * P:(g + 1) * P],
                                 xnT_hi[:, c, :], xnT_lo[:, c, :], c == 0, c == KT - 1)
                if KT - 1 in tiles:
                    last.then_inc(pj_ready, 1)

            def project_v(t, use, bank):
                pj_free(use)
                for c in range(KT):
                    last = three(ps_pj[bank][:], xnT_hi[:, c, t * P:(t + 1) * P], xnT_lo[:, c, t * P:(t + 1) * P],
                                 w_hi[2][:, c, :], w_lo[2][:, c, :], c == 0, c == KT - 1)
                last.then_inc(pj_ready, 1)

            def transpose_x(t, use, bank):
                pj_free(use)
                for c in range(KT):
                    last = nc.tensor.transpose(ps_pj[bank][:, c * P:(c + 1) * P], x_in[:, t % 2, c * P:(c + 1) * P], ident[:])
                last.then_inc(pj_ready, 1)

            def maxima_tile(g, u, n):
                j, t = u // TT, u % TT
                if not isinstance(n, int) or n >= 2:
                    pe.wait_ge(m_done, n - 1)
                nc.tensor.matmul(ps_m[u % 2][:], stacks[g][0:STACK, 0, j, t * P:(t + 1) * P], stacks[g][0:STACK, 1, j, :],
                                 start=True, stop=True).then_inc(m_ready, 1)

            def transpose_max(group):
                pe.wait_ge(m_done, UNITS * (group + 1))
                if not isinstance(group, int) or group >= 2:
                    pe.wait_ge(recip_done, group - 1)
                nc.tensor.transpose(ps_sum[0:UNITS, 0:P], neg_max_of(group), ident[:]).then_inc(maxT_ready, 1)

            def neg_max_of(group):
                return neg_max[:, GPAR[0], :]

            GPAR = [0]

            pe.wait_ge(lora_loaded, 32)

            def lora(m, use):
                for c in range(KT):
                    if use >= 2:
                        pj_free(use)
                    nc.tensor.matmul(ps_pj[use % 2][:], lb_sb[0:RANK, m, c * P:(c + 1) * P], la_sb[0:RANK, m, :],
                                     start=True, stop=True).then_inc(pj_ready, 1)
                    use += 1

            for m in range(3):
                lora(m, KT * m)
            pe.wait_ge(consts_ready, 3)
            use = AT_LN
            for t in range(TT):
                pe.wait_ge(xn_ready, t + 1)
                transpose_x(t, use, use % 2)
                use += 1
            pe.wait_ge(pj_done, AT_QK)
            for g in range(3):
                for m in range(2):
                    pe.wait_ge(w_lo_done, m + 1)
                    project_q(m, g, use, use % 2)
                    use += 1
            pe.wait_ge(w_lo_done, 3)
            for t in range(TT):
                project_v(t, use, use % 2)
                use += 1
            lora(3, AT_LORA_O)
            pe.wait_ge(stack_loaded[0], STACK_DMAS)
            for u in range(UNITS):
                maxima_tile(0, u, u)
            transpose_max(0)
            pe.wait_ge(w_lo_done, 4)
            pe.wait_ge(consts_ready, 3 + GROUPS)

            def body(b, first, last):
                for slot in range(GROUPS):
                    group = GROUPS * b + slot
                    nslot, nb = next_group(slot, b)
                    maxima = not (last and slot == GROUPS - 1)
                    m_next = 0
                    pe.wait_ge(row_loaded, 16 * (group + 1))
                    for u in range(UNITS):
                        kt, j = u // GH, u % GH
                        n = UNITS * group + u
                        if not (first and slot == 0 and u < 2):
                            pe.wait_ge(exp_done, n - 1)
                        s = nc.tensor.matmul(ps_s[u % 2][:], stacks[slot][0:STACK + 1, 1, j, kt * P:(kt + 1) * P],
                                             stacks[slot][0:STACK + 1, 0, j, :], start=True, stop=True)
                        s.then_inc(s_ready, 1)
                        if slot == 1 and not last and u in LN_AFTER:
                            t = LN_AFTER[u]
                            pe.wait_ge(xn_ready, TT * (b + 1) + t + 1)
                            transpose_x(t, *pj(b, "ln", 0, t))
                        if maxima:
                            for _ in range(M_AFTER[u]):
                                if m_next == 0:
                                    pe.wait_ge(stack_loaded[nslot], STACK_DMAS * (nb + 1))
                                maxima_tile(nslot, m_next, UNITS * (group + 1) + m_next)
                                m_next += 1
                        if u in (5, 9, 13):
                            weigh(b, slot, group, (u - 5) // GH)
                    project = slot == 0 or not last
                    if project:
                        if slot == 1:
                            pe.wait_ge(pj_done, pj(b, "ln", 0, TT - 1)[0] + 1)
                        project_q(0, (slot + 3) % GROUPS, *pj(b, "q", slot), range(0, 1))
                    if maxima:
                        GPAR[0] = (slot + 1) % 2
                        transpose_max(group + 1)
                    weigh(b, slot, group, KK - 1)
                    if maxima:
                        pe.wait_ge(maxT_done, group + 2)
                    else:
                        pe.wait_ge(recip_done, group)
                    pe.wait_ge(psum_added, 2 * GH * (group + 1))
                    for j in range(GH):
                        nc.tensor.matmul(ps_sum[j * HD:(j + 1) * HD, :], ones[:], p_sum[:, j, :], start=True, stop=False)
                        last_mm = nc.tensor.matmul(ps_sum[j * HD:(j + 1) * HD, :], ones[:], probs[:, (KK - 1) % 2, j, :],
                                                   start=False, stop=True)
                    last_mm.then_inc(sum_ready, 1)
                    if project:
                        project_q(0, (slot + 3) % GROUPS, *pj(b, "q", slot), range(1, KT))
                        project_q(1, (slot + 3) % GROUPS, *pj(b, "k", slot))
                    if slot == 0 and not last:
                        pe.wait_ge(xn_ready, TT * (b + 1) + 1)
                        transpose_x(0, *pj(b, "ln", 0, 0))
                if not last:
                    for t in range(TT):
                        project_v(t, *pj(b, "v", 0, t))
                pe.wait_ge(oT_lo_done, GROUPS * (b + 1))
                for t in range(TT):
                    o_use, bank = pj(b, "o", 0, t)
                    pj_free(o_use)
                    for g in range(GROUPS):
                        last_mm = three(ps_pj[bank][:], oT_hi[:, g, t * P:(t + 1) * P], oT_lo[:, g, t * P:(t + 1) * P],
                                        w_hi[3][:, g, :], w_lo[3][:, g, :], g == 0, g == GROUPS - 1)
                    last_mm.then_inc(pj_ready, 1)

            def weigh(b, slot, group, kt):
                pe.wait_ge(exp_done, UNITS * group + GH * (kt + 1))
                if kt == 0:
                    if not isinstance(group, int) or group >= 1:
                        pe.wait_ge(o_raw_done, group)
                    if slot == 0:
                        v_at = AT_LORA_O - 1 if isinstance(b, int) and b == 0 else pj(b - 1, "v", 0, TT - 1)[0]
                        pe.wait_ge(pj_done, v_at + 1)
                for j in range(GH):
                    head = slot * GH + j
                    mm = nc.tensor.matmul(ps_o[j * HD:(j + 1) * HD, :], v_sb[:, kt, head * HD:(head + 1) * HD],
                                          probs[:, kt % 2, j, :], start=kt == 0, stop=kt == KK - 1)
                mm.then_inc(pv_done, 1)

            per_batch(body, pe, pe.Fori)

            def transpose_xn2(c):
                for t in range(TT):
                    if c == 0 and t == 0:
                        pe.wait_ge(pj_done, pj(LAST, "o", 0, TT - 1)[0] + 1)
                    if c >= 3:
                        pe.wait_ge(y_done, TT * (c - 3) + t + 1)
                    pe.wait_ge(xn2_ready, TT * c + t + 1)
                    for k in range(KT):
                        mm = nc.tensor.transpose(ps_y[t][:, k * P:(k + 1) * P], xn2[:, t, k * P:(k + 1) * P], ident[:])
                    mm.then_inc(xn2T_ready, 1)

            def down(q, s, c):
                if c == 0:
                    pe.wait_ge(ffw_lo, 5 * s + 5)
                pe.wait_ge(hT_lo_done, q + 1)
                pe.wait_ge(hT_hi_done, q + 1)
                for t in range(TT):
                    if not isinstance(q, int) or q >= 1:
                        pe.wait_ge(y_done, TT * (q - 1) + t + 1)
                    for j in range(J):
                        mm = three(ps_y[t][:], hT_hi[:, j, t * P:(t + 1) * P], hT_lo[:, j, t * P:(t + 1) * P],
                                   dn_hi[:, j, :], dn_lo[:, j, :], j == 0, j == J - 1)
                    mm.then_inc(down_ready, 1)

            transpose_xn2(0)

            def block_step(s, first, last):
                for c in range(BATCHES):
                    q = BATCHES * s + c
                    if first:
                        pe.wait_ge(xn2T_done, TT * (c + 1))
                    for j in range(J):
                        n = J * q + j
                        if c == 0:
                            pe.wait_ge(ffw_lo, 5 * s + j + 1)
                        for part, (dst, freed, ready) in enumerate(((ps_gate, silu_done, gate_ready), (ps_up, h_ready, up_ready))):
                            if not first or n >= 2:
                                pe.wait_ge(freed, n - 1)
                            for k in range(KT):
                                mm = three(dst[j % 2][:], gu_hi[:, j, part, k * P:(k + 1) * P], gu_lo[:, j, part, k * P:(k + 1) * P],
                                           xn2T_hi[:, k, c * L:(c + 1) * L], xn2T_lo[:, k, c * L:(c + 1) * L],
                                           k == 0, k == KT - 1)
                            mm.then_inc(ready, 1)
                        if first and j == 1 and c < BATCHES - 1:
                            transpose_xn2(c + 1)
                    if first and c >= 1:
                        pe.wait_ge(xn2T_done, min(TT * (c + 2), NT))
                    if c:
                        down(q - 1, s, c - 1)
                    elif not first:
                        down(q - 1, s - 1, BATCHES - 1)

            per_block(block_step, pe.Fori)
            down(NT - 1, SB - 1, BATCHES - 1)

        @block.gpsimd
        def _(pool):
            nc.gpsimd.memset(ident[:], 0.0).then_inc(ident_zeroed, 1)
            nc.gpsimd.memset(neg_half[:], -0.5).then_inc(consts_ready, 1)
            nc.gpsimd.memset(ones[:], 1.0).then_inc(consts_ready, 1)
            pool.wait_ge(ident_zeroed, 1)
            nc.gpsimd.affine_select(out=ident[:], in_=ident[:], compare_op=ALU.not_equal, fill=1.0, base=0,
                                    pattern=[[-1, P]], channel_multiplier=1).then_inc(consts_ready, 1)

            def inverse_deviation(b):
                pool.wait_ge(var_ready, b + 1)
                at = slice(b * TT, (b + 1) * TT)
                nc.gpsimd.tensor_tensor(rstd[:, at], var_eps[:, at], neg_half[:, at], ALU.pow).then_inc(rstd_ready, 1)

            def weight_lo(m):
                pool.wait_ge(w_hi_done, m + 1)
                nc.gpsimd.tensor_tensor(w_lo[m][:], w_raw[m][:], w_hi[m][:].bitcast(F32), ALU.subtract).then_inc(w_lo_done, 1)

            pool.wait_ge(consts_ready, 3)
            inverse_deviation(0)
            for m in range(3):
                weight_lo(m)
            pool.wait_ge(w_lo_done, 3)
            for g in range(GROUPS):
                if g:
                    pool.wait_ge(consts_ready, 3 + g)
                nc.gpsimd.memset(stacks[g][STACK:STACK + 1, 1, :, :].bitcast(F32), 1.0).then_inc(consts_ready, 1)
            pool.wait_ge(consts_ready, 3 + GROUPS)
            for b in range(1, BATCHES):
                inverse_deviation(b)
            weight_lo(3)

            def body(b, first, last):
                for slot in range(GROUPS):
                    group = GROUPS * b + slot
                    for kt in range(1, KK - 1):
                        for j in range(GH):
                            pool.wait_ge(exp_done, UNITS * group + GH * kt + j + 1)
                            if kt == 1:
                                if not isinstance(group, int) or group >= 1:
                                    pool.wait_ge(sum_ready, group)
                                a = probs[:, 0, j, :]
                            else:
                                pool.wait_ge(psum_added, 2 * GH * group + GH * (kt - 2) + j + 1)
                                a = p_sum[:, j, :]
                            nc.gpsimd.tensor_tensor(p_sum[:, j, :], a, probs[:, kt % 2, j, :], ALU.add).then_inc(psum_added, 1)
                if first:
                    pool.wait_ge(bias_loaded, 32)
                for t in range(TT):
                    pool.wait_ge(x_res_loaded[t % 2], 32 * b + 16 * (t // 2 + 1))
                    nc.gpsimd.tensor_tensor(x_res[:, t % 2, :], x_res[:, t % 2, :], bo_sb[:], ALU.add).then_inc(x_res_ready, 1)

            per_batch(body, pool, pool.Fori)

            def split_gu(s, j):
                pool.wait_ge(ffw_hi, 5 * s + j + 1)
                nc.gpsimd.tensor_tensor(gu_lo[:, j], gu_raw[:, j], gu_hi[:, j].bitcast(F32), ALU.subtract).then_inc(ffw_lo, 1)

            def split_dn(s):
                pool.wait_ge(ffw_hi, 5 * s + 5)
                nc.gpsimd.tensor_tensor(dn_lo[:], dn_raw[:], dn_hi[:].bitcast(F32), ALU.subtract).then_inc(ffw_lo, 1)

            def pow2(c):
                pool.wait_ge(var2_ready, c + 1)
                nc.gpsimd.tensor_tensor(rstd[:, 0:TT], var_eps[:, 0:TT], neg_half[:, 0:TT], ALU.pow).then_inc(rstd2_ready, 1)

            for j in range(J):
                split_gu(0, j)
            pow2(0)
            split_dn(0)
            for c in range(1, BATCHES):
                pow2(c)

            def block_step(s, first, last):
                if not first:
                    split_dn(s)
                if not last:
                    for j in range(J):
                        split_gu(s + 1, j)

            per_block(block_step, pool.Fori)

        @block.scalar
        def _(act):
            def hi_of(dst, src, bias_col=None):
                if bias_col is None:
                    return nc.scalar.activation(dst, src, ACT.Copy)
                return nc.scalar.activation(dst, src, ACT.Identity, bias=bias_col)

            def xnT_part(t, use, bank):
                act.wait_ge(pj_ready, use + 1)
                hi_of(xnT_hi[:, :, t * P:(t + 1) * P],
                      ps_pj[bank][:].rearrange("p (c n) -> p c n", c=KT)).then_inc(xnT_hi_done, 1)

            def qk_part(m, g, use, bank):
                act.wait_ge(pj_ready, use + 1)
                hi_of(qk_parts[:, (Q_HI, K_HI)[m], :], ps_pj[bank][:], bias[:, m, g:g + 1]).then_inc(qk_hi_done, 1)

            def max_row(slot, group):
                act.wait_ge(maxT_ready, group + 1)
                if not isinstance(group, int) or group >= 1:
                    act.wait_ge(row_loaded, 16 * group)
                hi_of(row_max[0:UNITS, :], ps_sum[0:UNITS, 0:P]).then_inc(maxT_done, 1)
                act.wait_ge(maxT_done, group + 1)
                act.dma_start(stacks[slot][STACK:STACK + 1, 0, :, :].bitcast(F32), row_max[0:UNITS, :].bitcast(F32))\
                   .then_inc(row_loaded, 16)

            def weight_hi(m):
                act.wait_ge(pj_done, KT * (m + 1) if m < 3 else PJ_START)
                hi_of(w_hi[m][:], w_raw[m][:]).then_inc(w_hi_done, 1)

            weight_hi(0)
            weight_hi(1)
            weight_hi(2)
            use = AT_LN
            for t in range(TT):
                xnT_part(t, use, use % 2)
                use += 1
            act.wait_ge(bias_loaded, 32)
            for g in range(3):
                for m in range(2):
                    if g:
                        act.wait_ge(stack_loaded[g - 1], STACK_DMAS)
                    qk_part(m, g, use, use % 2)
                    use += 1
            weight_hi(3)
            max_row(0, 0)

            def body(b, first, last):
                for slot in range(GROUPS):
                    group = GROUPS * b + slot
                    nslot, nb = next_group(slot, b)
                    maxima = not (last and slot == GROUPS - 1)
                    for u in range(UNITS):
                        kt, j = u // GH, u % GH
                        n = UNITS * group + u
                        act.wait_ge(s_ready, n + 1)
                        if not (first and slot == 0 and kt < 2):
                            if j == 0:
                                act.wait_ge(pv_done, KK * group + kt - 1)
                            if kt == 1:
                                if j == 0:
                                    act.wait_ge(sum_ready, group)
                            else:
                                act.wait_ge(psum_added, 2 * GH * group + (j + 1 if kt else j + 1 - GH))
                        nc.scalar.activation(probs[:, kt % 2, j, :], ps_s[u % 2][:], ACT.Exp, scale=SCALE).then_inc(exp_done, 1)
                        if slot == 1 and not last and u in LN_AFTER:
                            xnT_part(LN_AFTER[u], *pj(b, "ln", 0, LN_AFTER[u]))
                    if maxima:
                        max_row(nslot, group + 1)
                    if slot == 0 or not last:
                        prev = (slot + 2) % GROUPS
                        act.wait_ge(stack_loaded[prev], STACK_DMAS * (b + (1 if slot < 2 else 2)))
                        qk_part(0, (slot + 3) % GROUPS, *pj(b, "q", slot))
                        qk_part(1, (slot + 3) % GROUPS, *pj(b, "k", slot))
                    if slot == 0 and not last:
                        xnT_part(0, *pj(b, "ln", 0, 0))
                    if last and slot == 2:
                        ffn_weights(0)
                act.wait_ge(o_raw_done, GROUPS * (b + 1))
                for g in range(GROUPS):
                    hi_of(oT_hi[:, g, :], o_raw[:, g, :], bias[:, 2, g:g + 1]).then_inc(oT_hi_done, 1)

            def gu_hi_part(s, j):
                act.wait_ge(gu_loaded[j], 16 * (s + 1))
                hi_of(gu_hi[:, j], gu_raw[:, j]).then_inc(ffw_hi, 1)

            def dn_hi_part(s):
                act.wait_ge(dn_loaded, 16 * (s + 1))
                hi_of(dn_hi[:], dn_raw[:]).then_inc(ffw_hi, 1)

            def ffn_weights(s):
                for j in range(J):
                    gu_hi_part(s, j)
                dn_hi_part(s)

            per_batch(body, act, act.Fori)

            def xn2T_part(c):
                for t in range(TT):
                    act.wait_ge(xn2T_ready, TT * c + t + 1)
                    hi_of(xn2T_hi[:, :, c * L + t * P:c * L + (t + 1) * P],
                          ps_y[t][:].rearrange("p (c n) -> p c n", c=KT)).then_inc(xn2T_hi_done, 1)

            xn2T_part(0)

            def block_step(s, first, last):
                for c in range(BATCHES):
                    q = BATCHES * s + c

                    def gate(j):
                        n = J * q + j
                        act.wait_ge(gate_ready, n + 1)
                        if not first or n >= 2:
                            act.wait_ge(h_ready, n - 1)
                        nc.scalar.activation(silu[:, j % 2, :], ps_gate[j % 2][:], ACT.Silu).then_inc(silu_done, 1)

                    def size(j):
                        act.wait_ge(h_ready, J * q + j + 1)
                        if not first or c >= 1:
                            act.wait_ge(mask_step, 10 * (q - 1) + 3)
                        nc.scalar.activation(h_abs[:, j, :], h[:, j, :], ACT.Abs).then_inc(abs_done, 1)

                    gate(0)
                    gate(1)
                    if c == 1 and not first:
                        dn_hi_part(s)
                    size(0)
                    if first and c < BATCHES - 1:
                        xn2T_part(c + 1)
                    gate(2)
                    size(1)
                    gate(3)
                    size(2)
                    if c == BATCHES - 1 and not last:
                        gu_hi_part(s + 1, 0)
                        gu_hi_part(s + 1, 1)
                    size(3)
                    if c == BATCHES - 1 and not last:
                        gu_hi_part(s + 1, 2)
                        gu_hi_part(s + 1, 3)
                    if not first or c >= 1:
                        act.wait_ge(down_ready, TT * q)
                    act.wait_ge(h_kept, J * (q + 1))
                    hi_of(hT_hi[:], h[:]).then_inc(hT_hi_done, 1)

            per_block(block_step, act.Fori)

        @block.vector
        def _(dve):
            def statistics(src, step, var_sem, mean_at, loaded, count):
                dve.wait_ge(loaded, 16)
                for t in range(TT):
                    nc.vector.bn_stats(stats[:, t, :], src(t)).then_inc(step, 1)
                for t in range(TT):
                    dve.wait_ge(step, (2 * TT) * count + t + 1)
                    nc.vector.bn_aggr(mv[:, mean_at + t, :], stats[:, t, :]).then_inc(step, 1)
                dve.wait_ge(step, (2 * TT) * (count + 1))
                nc.vector.tensor_scalar(var_eps[:, mean_at:mean_at + TT], mv[:, mean_at:mean_at + TT, 1], EPS, None,
                                        ALU.add).then_inc(var_sem, 1)

            def normalise(dst, src, mean, r):
                return nc.vector.tensor_scalar(dst, src, mean, r, ALU.subtract, ALU.mult)

            def xnT_part(t, use, bank, n):
                dve.wait_ge(xnT_hi_done, n + 1)
                nc.vector.tensor_tensor(xnT_lo[:, :, t * P:(t + 1) * P],
                                        ps_pj[bank][:].rearrange("p (c n) -> p c n", c=KT),
                                        xnT_hi[:, :, t * P:(t + 1) * P].bitcast(F32), ALU.subtract).then_inc(pj_done, 1)

            def qk_part(m, g, bank, n):
                dve.wait_ge(qk_hi_done, n + 1)
                nc.vector.scalar_tensor_tensor(qk_parts[:, (Q_LO, K_LO)[m], :], ps_pj[bank][:], bias[:, m, g:g + 1],
                                               qk_parts[:, (Q_HI, K_HI)[m], :].bitcast(F32), ALU.add, ALU.subtract).then_inc(pj_done, 1)

            def v_part(t, use, bank):
                dve.wait_ge(pj_ready, use + 1)
                nc.vector.tensor_copy(v_sb[:, t, :], ps_pj[bank][:]).then_inc(pj_done, 1)

            def reduce(u, n, par):
                dve.wait_ge(m_ready, n + 1)
                nc.vector.tensor_reduce(neg_max[:, par, u:u + 1], ps_m[u % 2][:], AX.X, ALU.max, negate=True).then_inc(m_done, 1)

            def lora_part(m, use):
                dve.wait_ge(w_loaded[m], 16)
                for c in range(KT):
                    dve.wait_ge(pj_ready, use + c + 1)
                    nc.vector.scalar_tensor_tensor(w_raw[m][:, c, :], ps_pj[(use + c) % 2][:], LORA, w_raw[m][:, c, :],
                                                   ALU.mult, ALU.add).then_inc(pj_done, 1)

            def batch_statistics(b):
                statistics(lambda t: x_all[:, b * TT + t, :], stats_step, var_ready, b * TT, x_loaded[b], b)

            batch_statistics(0)
            lora_part(0, 0)
            dve.wait_ge(rstd_ready, 1)
            for t in range(2):
                normalise(x_in[:, t, :], x_all[:, t, :], mv[:, t, 0:1], rstd[:, t:t + 1]).then_inc(xn_ready, 1)
            for m in range(1, 3):
                lora_part(m, KT * m)
            use = AT_LN
            for t in range(TT):
                xnT_part(t, use, use % 2, t)
                if t < 2:
                    normalise(x_in[:, t, :], x_all[:, t + 2, :], mv[:, t + 2, 0:1], rstd[:, t + 2:t + 3]).then_inc(xn_ready, 1)
                use += 1
            dve.wait_ge(bias_loaded, 32)
            for g in range(3):
                for m in range(2):
                    qk_part(m, g, use % 2, 2 * g + m)
                    use += 1
                batch_statistics(g + 1)
            for t in range(TT):
                v_part(t, use, use % 2)
                use += 1
            lora_part(3, AT_LORA_O)
            for u in range(UNITS):
                reduce(u, u, 0)

            def body(b, first, last):
                for slot in range(GROUPS):
                    group = GROUPS * b + slot
                    maxima = not (last and slot == GROUPS - 1)
                    m_next = 0
                    if slot == 0 and first:
                        dve.wait_ge(rstd_ready, BATCHES)
                    for u in range(UNITS):
                        if slot == 1 and not last and u in LN_AFTER:
                            t = LN_AFTER[u]
                            ln_use, bank = pj(b, "ln", 0, t)
                            xnT_part(t, ln_use, bank, TT * (b + 1) + t)
                        if slot < 2 and not last and u in (6, 7):
                            next_tile(b, 2 * slot + u - 6)
                        if maxima:
                            for _ in range(M_AFTER[u]):
                                reduce(m_next, UNITS * (group + 1) + m_next, (slot + 1) % 2)
                                m_next += 1
                    dve.wait_ge(sum_ready, group + 1)
                    nc.vector.reciprocal(recip[:], ps_sum[:]).then_inc(recip_done, 1)
                    dve.wait_ge(recip_done, group + 1)
                    if slot == 0 and not first:
                        dve.wait_ge(oT_hi_done, GROUPS * b)
                    nc.vector.tensor_tensor(o_raw[:, slot, :], ps_o[:], recip[:], ALU.mult).then_inc(o_raw_done, 1)
                    if slot == 0 or not last:
                        for m, what in enumerate("qk"):
                            qk_part(m, (slot + 3) % GROUPS, pj(b, what, slot)[1], 6 + 8 * b + 2 * slot + m)
                    if slot == 0 and not last:
                        xnT_part(0, *pj(b, "ln", 0, 0), TT * (b + 1))
                for g in range(GROUPS):
                    if not last and g < 3:
                        v_part(g, *pj(b, "v", 0, g))
                    dve.wait_ge(oT_hi_done, GROUPS * b + g + 1)
                    nc.vector.scalar_tensor_tensor(oT_lo[:, g, :], o_raw[:, g, :], bias[:, 2, g:g + 1],
                                                   oT_hi[:, g, :].bitcast(F32), ALU.add, ALU.subtract).then_inc(oT_lo_done, 1)
                if not last:
                    v_part(3, *pj(b, "v", 0, 3))
                for t in range(TT):
                    o_use, bank = pj(b, "o", 0, t)
                    dve.wait_ge(pj_ready, o_use + 1)
                    dve.wait_ge(x_res_ready, TT * b + t + 1)
                    nc.vector.tensor_tensor(x_res[:, t % 2, :], ps_pj[bank][:], x_res[:, t % 2, :], ALU.add).then_inc(pj_done, 1)

            def next_tile(b, t):
                at = (b + 1) * TT + t
                dve.wait_ge(x_in_loaded[t % 2], 32 * b + 16 * (t // 2 + 1))
                normalise(x_in[:, t % 2, :], x_in[:, t % 2, :], mv[:, bass.ds(at, 1), 0], rstd[:, bass.ds(at, 1)]).then_inc(xn_ready, 1)

            per_batch(body, dve, dve.Fori)

            def norm2(c):
                statistics(lambda t: y[:, c * TT + t, :], stats2_step, var2_ready, 0, x2_back[c], c)
                dve.wait_ge(rstd2_ready, c + 1)
                for t in range(TT):
                    if c:
                        dve.wait_ge(xn2T_ready, TT * (c - 1) + t + 1)
                    normalise(xn2[:, t, :], y[:, c * TT + t, :], mv[:, t, 0:1], rstd[:, t:t + 1]).then_inc(xn2_ready, 1)

            def xn2T_part(c):
                for t in range(TT):
                    dve.wait_ge(xn2T_hi_done, TT * c + t + 1)
                    at = slice(c * L + t * P, c * L + (t + 1) * P)
                    nc.vector.tensor_tensor(xn2T_lo[:, :, at], ps_y[t][:].rearrange("p (c n) -> p c n", c=KT),
                                            xn2T_hi[:, :, at].bitcast(F32), ALU.subtract).then_inc(xn2T_done, 1)

            norm2(0)
            xn2T_part(0)

            def add_down(q, c):
                for t in range(TT):
                    dve.wait_ge(down_ready, TT * q + t + 1)
                    nc.vector.tensor_tensor(y[:, c * TT + t, :], ps_y[t][:], y[:, c * TT + t, :], ALU.add).then_inc(y_done, 1)

            def block_step(s, first, last):
                for c in range(BATCHES):
                    q = BATCHES * s + c
                    if first and c < BATCHES - 1:
                        norm2(c + 1)
                    for j in range(J):
                        n = J * q + j
                        dve.wait_ge(up_ready, n + 1)
                        dve.wait_ge(silu_done, n + 1)
                        if j == 0 and not (first and c == 0):
                            dve.wait_ge(hT_hi_done, q)
                            dve.wait_ge(hT_lo_done, q)
                        nc.vector.tensor_tensor(h[:, j, :], ps_up[j % 2][:], silu[:, j % 2, :], ALU.mult).then_inc(h_ready, 1)
                        if first and j == 1 and c < BATCHES - 1:
                            xn2T_part(c + 1)
                    step = 10 * q
                    dve.wait_ge(abs_done, J * (q + 1))
                    nc.vector.tensor_tensor(pair_max[:], h_abs[:, 0:J:2, :], h_abs[:, 1:J:2, :], ALU.max).then_inc(mask_step, 1)
                    nc.vector.tensor_tensor(pair_min[:], h_abs[:, 0:J:2, :], h_abs[:, 1:J:2, :], ALU.min).then_inc(mask_step, 1)
                    nc.vector.tensor_tensor(first_wins[:], h_abs[:, 0:J:2, :], h_abs[:, 1:J:2, :], ALU.is_ge).then_inc(mask_step, 1)
                    dve.wait_ge(mask_step, step + 2)
                    nc.vector.tensor_tensor(both_01[:], pair_min[:, 0, :], pair_max[:, 1, :], ALU.is_ge).then_inc(mask_step, 1)
                    nc.vector.tensor_tensor(both_23[:], pair_min[:, 1, :], pair_max[:, 0, :], ALU.is_gt).then_inc(mask_step, 1)
                    dve.wait_ge(mask_step, step + 5)
                    nc.vector.tensor_tensor(tilt[:], both_01[:], both_23[:], ALU.subtract).then_inc(mask_step, 1)
                    dve.wait_ge(mask_step, step + 6)
                    for i in range(2):
                        nc.vector.tensor_tensor(wins_up[:, i, :], first_wins[:, i, :], tilt[:], ALU.add).then_inc(mask_step, 1)
                        nc.vector.tensor_tensor(wins_down[:, i, :], first_wins[:, i, :], tilt[:], ALU.subtract).then_inc(mask_step, 1)
                    dve.wait_ge(mask_step, step + 10)
                    kept = ((wins_up, 0, ALU.is_ge, 1.0), (wins_down, 0, ALU.is_le, 0.0),
                            (wins_down, 1, ALU.is_ge, 1.0), (wins_up, 1, ALU.is_le, 0.0))
                    for j, (wins, i, op, bound) in enumerate(kept):
                        nc.vector.scalar_tensor_tensor(h[:, j, :], wins[:, i, :], bound, h[:, j, :], op, ALU.mult).then_inc(h_kept, 1)
                    dve.wait_ge(hT_hi_done, q + 1)
                    nc.vector.tensor_tensor(hT_lo[:], h[:], hT_hi[:].bitcast(F32), ALU.subtract).then_inc(hT_lo_done, 1)
                    if c:
                        add_down(q - 1, c - 1)
                    elif not first:
                        add_down(q - 1, BATCHES - 1)

            per_block(block_step, dve.Fori)
            add_down(NT - 1, BATCHES - 1)


def kernel(**inputs):
    import numpy as np
    import concourse.bacc as bacc
    from concourse.bass_utils import run_bass_kernel_spmd

    a = {k.replace("L0_attn_", "").replace("L0_ffn_", ""): np.asarray(v) for k, v in inputs.items()}
    names = "qkvo"
    arrays = {
        "x_in": a["x"].reshape(NT, P, D).transpose(1, 0, 2),
        "wqkvo_in": np.stack([a["W" + n].T.reshape(KT, P, D).transpose(1, 0, 2) for n in names]),
        "lora_b_in": np.stack([a["B" + n] for n in names], axis=1),
        "lora_a_in": np.stack([a["A" + n].T for n in names], axis=1),
        "bias_cols_in": np.stack([a["b" + n].reshape(KT, P).T for n in "qkv"], axis=1),
        "bo_rows_in": np.broadcast_to(a["bo"], (P, D)),
        "w_gu_in": np.stack([a["w_" + n].reshape(KT, P, SB, P, J).transpose(1, 2, 4, 0, 3) for n in ("gate", "up")], axis=3)
                     .reshape(P, SB, J, 2, KT * P),
        "w_down_in": a["w_down"].reshape(SB, P, J, D).transpose(1, 0, 2, 3),
    }
    arrays = {k: np.ascontiguousarray(v) for k, v in arrays.items()}
    nc = bacc.Bacc("TRN2", target_bir_lowering=False, num_devices=1)
    args = [nc.dram_tensor(k, v.shape, mybir.dt.from_np(v.dtype), kind="ExternalInput").ap() for k, v in arrays.items()]
    out = nc.dram_tensor("x_out", (P, NT, D), F32, kind="ExternalOutput").ap()
    block_kernel(nc, *args, out)
    r = run_bass_kernel_spmd(nc, [arrays], core_ids=[0])
    got = r.results[0]["x_out"]
    return np.ascontiguousarray(got.transpose(1, 0, 2)).reshape(BATCHES, L, D)
```

```python
from contextlib import ExitStack

import concourse.bass as bass
import concourse.mybir as mybir

P = 128
F32 = mybir.dt.float32
F32R = mybir.dt.float32r
BF16 = mybir.dt.bfloat16
ALU = mybir.AluOpType
ACT = mybir.ActivationFunctionType
AX = mybir.AxisListType

BATCHES, L, D = 4, 512, 512
HEADS, HD, RANK = 16, 32, 16
FF = 2048
KT = D // P
TT = L // P
KK = L // P
GH = P // HD
GROUPS = HEADS // GH
NT = BATCHES * TT
J = 4
SB = FF // (J * P)
LORA = 8.0 / RANK
SCALE = HD ** -0.5
EPS = 1e-5
STACK = 3 * HD
UNITS = KK * GH
LAST = BATCHES - 1

PJ_LN, PJ_V, PJ_O = TT, TT, TT
AT_LN = 0
AT_Q0 = AT_LN + PJ_LN
AT_V = AT_Q0 + 2
AT_Q1 = AT_V + PJ_V
AT_Q = (AT_Q0, AT_Q1, AT_Q1 + 2)
PJ_START = AT_Q1 + 4
PJ_BODY = 2 * GROUPS + PJ_LN + PJ_V + PJ_O
STACK_DMAS = 16 * 3 * GH

M_AFTER = [0] + [1] * 14 + [2]
LN_AFTER = {12: 2, 13: 3}
STATS_AFTER, NORMALISE_AFTER = ((8, 9, 10), (4, 5, 6)), (14, 10)


def pj_use(what, slot=0):
    if what in ("q", "k"):
        return (0, 6, 8, 10)[slot] + (what == "k")
    return {"ln": 2, "v": 12, "o": 16}[what]


def block_kernel(nc, x, wqkvo, lora_b, lora_a, bias_cols, bo_rows, w_gu, w_down, out):
    x2_dram = nc.dram_tensor("x2_dram", [NT, P, D], F32, kind="Internal").ap()
    x2_flat = x2_dram.rearrange("t p d -> (t p d)")
    x_rows = x.rearrange("p t d -> p (t d)")
    w_gu_rows = w_gu.rearrange("p s j a n -> p (s j a n)")
    w_down_rows = w_down.rearrange("p s j d -> p (s j d)")
    start = -(-nc.sbuf_base // 64) * 64

    with ExitStack() as ctx:
        def sb(name, at_kb, shape, dt=F32):
            return nc.alloc_sbuf_tensor_at(name, [P] + shape, dt, offset=start + int(at_kb * 1024))

        def sem(name):
            return ctx.enter_context(nc.semaphore(name))

        w_hi = [sb(f"w_hi_{n}", 16 * i, [KT, D], F32R) for i, n in enumerate("qkvo")]
        w_lo = [sb(f"w_lo_{n}", 16 * i + 8, [KT, D], F32R) for i, n in enumerate("qkvo")]
        w_raw = [sb(f"w_raw_{n}", 16 * i + 8, [KT, D]) for i, n in enumerate("qkvo")]
        xnT_hi = sb("xnT_hi", 64, [KT, L], F32R)
        xnT_lo = sb("xnT_lo", 72, [KT, L], F32R)
        qk_parts = sb("qk_parts", 80, [4, L], F32R)
        Q_HI, Q_LO, K_LO, K_HI = range(4)
        qk_parts1 = sb("qk_parts1", 128, [4, L], F32R)
        x_in = sb("x_in", 88, [2, D])
        y = sb("y", 64, [NT, D])
        x_res = y[:, LAST * TT:, :]
        probs = sb("probs", 96, [2, GH, L])
        oT_hi = sb("oT_hi", 96, [GROUPS, L], F32R)
        oT_lo = sb("oT_lo", 104, [GROUPS, L], F32R)
        x_first = sb("x_first", 96, [TT, D])
        p_sum = sb("p_sum", 112, [GH, L])
        v_sb = sb("v_sb", 120, [KK, D])
        o_raw = sb("o_raw", 128, [GROUPS, L])
        recip = sb("recip", 136, [L])
        bo_sb = sb("bo_sb", 138, [D])
        stacks = [sb(f"stack{g}", 140 + 16 * g, [2, GH, L], F32R) for g in range(GROUPS)]
        lora_stack = sb("lora_stack", 172, [2, 4, D], F32R)
        lora_raw = sb("lora_raw", 188, [2, 4, D])
        ident = sb("ident", 204, [P])
        row_max = sb("row_max", 204.5, [P], F32R)
        stats = sb("stats", 205, [4, 6])
        mv = sb("mv", 205.25, [TT, 2])
        rstd = sb("rstd", 205.5, [TT])
        neg_half = sb("neg_half", 205.75, [TT])
        var_eps = sb("var_eps", 206, [TT])
        neg_max = sb("neg_max", 206.25, [2, UNITS])
        bias = sb("bias", 206.5, [3, KT])
        ones = sb("ones", 206.75, [HD])

        gu_hi = sb("gu_hi", 0, [J, 2, KT * P], F32R)
        gu_lo = sb("gu_lo", 16, [J, 2, KT * P], F32R)
        gu_raw = sb("gu_raw", 16, [J, 2, KT * P])
        dn_hi = sb("dn_hi", 32, [J, D], F32R)
        dn_lo = sb("dn_lo", 40, [J, D], F32R)
        dn_raw = sb("dn_raw", 40, [J, D])
        h = sb("h", 48, [J, L])
        h_abs = sb("h_abs", 56, [J, L])
        hT_hi = sb("hT_hi", 96, [J, L], F32R)
        hT_lo = sb("hT_lo", 104, [J, L], F32R)
        silu = sb("silu", 112, [2, L])
        pair_max = sb("pair_max", 116, [2, L])
        pair_min = sb("pair_min", 120, [2, L])
        first_wins = sb("first_wins", 124, [2, L], BF16)
        both_01 = sb("both_01", 126, [L], BF16)
        both_23 = sb("both_23", 127, [L], BF16)
        tilt = sb("tilt", 130, [L], BF16)
        wins_up = sb("wins_up", 126, [2, L], BF16)
        wins_down = sb("wins_down", 128, [2, L], BF16)
        xn2 = sb("xn2", 132, [TT, D])
        xn2T_hi = sb("xn2T_hi", 140, [KT, NT * P], F32R)
        xn2T_lo = sb("xn2T_lo", 172, [KT, NT * P], F32R)

        banks = [ctx.enter_context(nc.psum_tensor(f"bank{i}", [P, 512], F32)) for i in range(8)]
        ps_s, ps_m, ps_pj, ps_o, ps_sum = banks[0:2], banks[2:4], banks[4:6], banks[6], banks[7]
        ps_lora = [banks[i] for i in (0, 1, 6, 7, 2, 3)]
        ps_gate, ps_up, ps_y = banks[0:2], banks[2:4], banks[4:8]

        w_loaded = [sem(f"w_loaded_{n}") for n in "qkvo"]
        x_first_loaded = sem("x_first_loaded")
        lora_loaded, bias_loaded, bo_loaded = sem("lora_loaded"), sem("bias_loaded"), sem("bo_loaded")
        consts_ready, ident_zeroed = sem("consts_ready"), sem("ident_zeroed")
        lora_ready, lora_done = sem("lora_ready"), sem("lora_done")
        lora_zeroed = [sem(f"lora_zeroed{side}") for side in range(2)]
        lora_hi, lora_lo = sem("lora_hi"), [sem(f"lora_lo{half}") for half in range(2)]
        stats_step, var_ready, rstd_ready = sem("stats_step"), sem("var_ready"), sem("rstd_ready")
        w_hi_done, w_lo_done = [[sem(f"w_{part}_done_{n}") for n in "qkvo"] for part in ("hi", "lo")]
        x_in_loaded = [sem(f"x_in_loaded{i}") for i in range(2)]
        xn_ready = sem("xn_ready")
        pj_ready, pj_done = sem("pj_ready"), sem("pj_done")
        xnT_hi_done, qk_hi_done = sem("xnT_hi_done"), sem("qk_hi_done")
        stack_loaded = [sem(f"stack_loaded{g}") for g in range(GROUPS)]
        row_loaded = sem("row_loaded")
        m_ready, m_done = sem("m_ready"), sem("m_done")
        maxT_ready, maxT_done = sem("maxT_ready"), sem("maxT_done")
        s_ready, exp_done = sem("s_ready"), sem("exp_done")
        pv_done, psum_added = sem("pv_done"), sem("psum_added")
        sum_ready, recip_done, o_raw_done = sem("sum_ready"), sem("recip_done"), sem("o_raw_done")
        oT_hi_done, oT_lo_done = sem("oT_hi_done"), sem("oT_lo_done")
        x_res_loaded = sem("x_res_loaded")
        x_res_ready = sem("x_res_ready")
        x2_stored = [sem(f"x2_stored{i}") for i in range(2)]

        gu_loaded = [sem(f"gu_loaded{j}") for j in range(J)]
        dn_loaded = sem("dn_loaded")
        ffw_hi, ffw_lo = sem("ffw_hi"), sem("ffw_lo")
        x2_back = [sem(f"x2_back{c}") for c in range(LAST)]
        stats2_step, var2_ready, rstd2_ready = sem("stats2_step"), sem("var2_ready"), sem("rstd2_ready")
        xn2_ready, xn2T_ready = sem("xn2_ready"), sem("xn2T_ready")
        xn2T_hi_done, xn2T_done = sem("xn2T_hi_done"), sem("xn2T_done")
        gate_ready, up_ready = sem("gate_ready"), sem("up_ready")
        silu_done, h_ready, abs_done = sem("silu_done"), sem("h_ready"), sem("abs_done")
        mask_step, h_kept = sem("mask_step"), sem("h_kept")
        hT_hi_done, hT_lo_done = sem("hT_hi_done"), sem("hT_lo_done")
        down_ready, y_done = sem("down_ready"), sem("y_done")
        out_stored = sem("out_stored")

        def per_batch(body, eng, loop):
            body(0, True, False)
            with loop(1, LAST) as b:
                body(b, False, False)
            body(LAST, False, True)

        def per_block(step, loop):
            step(0, True, False)
            with loop(1, SB - 1) as s:
                step(s, False, False)
            step(SB - 1, False, True)

        def split_lora_lo(eng, ops, half):
            for side, copy in enumerate((2, 1)):
                eng.wait_ge(lora_hi, 2 * half + side + 1)
                if half and side:
                    eng.wait_ge(lora_lo[1], 1)
                rows, ms = slice(copy * HD, (copy + 1) * HD), slice(2 * half, 2 * half + 2)
                ops.tensor_tensor(lora_stack[rows, side, ms], lora_raw[rows, side, ms],
                                  lora_stack[rows, side, ms].bitcast(F32), ALU.subtract).then_inc(lora_lo[half], 1)

        def next_group(slot, b):
            return (slot + 1, b) if slot < GROUPS - 1 else (0, b + 1)

        def pj(b, what, slot=0, t=0):
            n = pj_use(what, slot)
            if isinstance(b, int) and b == LAST and what == "o":
                n = 2
            return PJ_START + PJ_BODY * b + n + t, (n + t) % 2

        block = ctx.enter_context(nc.Block())

        @block.sync
        def _(sp):
            sp.dma_start(x_first[:], x[:, 0:TT, :]).then_inc(x_first_loaded, 16)
            for side in range(2):
                sp.wait_ge(lora_zeroed[side], 1)
            for copy in range(3):
                for side, factor in enumerate((lora_b, lora_a)):
                    sp.dma_start(lora_raw[copy * HD:copy * HD + RANK, side], factor).then_inc(lora_loaded, 16)
            for m in range(4):
                sp.dma_start(w_raw[m][:], wqkvo[m]).then_inc(w_loaded[m], 16)
                if m == 0:
                    sp.dma_start(bias[:], bias_cols).then_inc(bias_loaded, 16)
            sp.dma_start(bo_sb[:], bo_rows).then_inc(bo_loaded, 16)

            def held(value):
                return value if isinstance(value, int) else sp.snap(value)

            def stack(g, split, parts=qk_parts):
                sp.wait_ge(pj_done, split)
                for j in range(GH):
                    for row, (of_q, of_k) in enumerate(((Q_HI, K_HI), (Q_HI, K_LO), (Q_LO, K_HI))):
                        sp.dma_start(stacks[g][row * HD:(row + 1) * HD, :, j, :].bitcast(F32),
                                     parts[j * HD:(j + 1) * HD, of_q:of_k + 1:of_k - of_q, :].bitcast(F32))\
                          .then_inc(stack_loaded[g], 16)

            def load_x_in(b, t, transposed):
                at = held(((b + 1) * TT + t) * D)
                sp.wait_ge(pj_ready, transposed)
                sp.dma_start(x_in[:, t % 2, :], x_rows[:, bass.ds(at, D)]).then_inc(x_in_loaded[t % 2], 16)

            for g in range(3):
                if g == 1:
                    for t in range(2):
                        load_x_in(0, t, AT_LN + TT)
                stack(g, AT_Q[g] + 2, qk_parts1 if g == 1 else qk_parts)

            def body(b, first, last):
                for slot in range(GROUPS):
                    if not last and slot == 0:
                        if not first:
                            sp.wait_ge(x2_stored[0], held(16 * b))
                        for t in range(2 if first else 0, TT):
                            load_x_in(b, t, held(pj(b, "ln", 0, t - 2)[0] + 1) if t >= 2 else
                                      held(pj(b - 1, "ln", 0, t + 2)[0] + 1))
                    if slot == (0 if last else 3):
                        transposed = held(pj(b - last, "ln", 0, TT - 1)[0] + 1)
                        at, stored = held(b * TT * D), held(16 * b)
                        sp.wait_ge(pj_ready, transposed)
                        if not first:
                            for i in range(2):
                                sp.wait_ge(x2_stored[i], stored)
                        sp.dma_start(x_res.rearrange("p t d -> p (t d)"), x_rows[:, bass.ds(at, TT * D)]).then_inc(x_res_loaded, 16)
                    if slot == 0 or not last:
                        stack((slot + 3) % GROUPS, held(pj(b, "k", slot)[0] + 1))
                    if last and slot == 1:
                        sp.wait_ge(pj_ready, pj(b, "k", 0)[0] + 1)
                        for j in range(J):
                            sp.dma_start(gu_raw[:, j], w_gu[:, 0, j]).then_inc(gu_loaded[j], 16)
                        sp.dma_start(dn_raw[:], w_down[:, 0]).then_inc(dn_loaded, 16)
                        sp.wait_ge(stack_loaded[3], STACK_DMAS * BATCHES)
                        for c in range(BATCHES - 1):
                            sp.dma_start(y[:, c * TT:(c + 1) * TT, :],
                                         x2_dram[c * TT:(c + 1) * TT].rearrange("t p d -> p t d")).then_inc(x2_back[c], 16)
                if not last:
                    for i in range(2):
                        computed, at = held(pj(b, "o", 0, 2 * i + 1)[0] + 1), held((b * TT + 2 * i) * P * D)
                        sp.wait_ge(pj_done, computed)
                        sp.dma_start(x2_flat[bass.ds(at, 2 * P * D)].rearrange("(t p d) -> p t d", t=2, p=P),
                                     x_res[:, 2 * i:2 * i + 2, :]).then_inc(x2_stored[i], 16)

            per_batch(body, sp, sp.Fori)

            def block_step(s, first, last):
                if not first:
                    done, at = held(16 * s), held(s * J * D)
                    sp.wait_ge(down_ready, done)
                    sp.dma_start(dn_raw[:].rearrange("p j d -> p (j d)"), w_down_rows[:, bass.ds(at, J * D)]).then_inc(dn_loaded, 16)
                if not last:
                    for j in range(J):
                        done, at = held(16 * s + 12 + j + 1), held(((s + 1) * J + j) * 2 * KT * P)
                        sp.wait_ge(up_ready, done)
                        sp.dma_start(gu_raw[:, j].rearrange("p a n -> p (a n)"), w_gu_rows[:, bass.ds(at, 2 * KT * P)]).then_inc(gu_loaded[j], 16)

            per_block(block_step, sp.Fori)
            for c in range(BATCHES):
                sp.wait_ge(y_done, NT * (SB - 1) + TT * (c + 1))
                sp.dma_start(out[:, c * TT:(c + 1) * TT, :], y[:, c * TT:(c + 1) * TT, :]).then_inc(out_stored, 16)
            sp.wait_ge(out_stored, 16 * BATCHES)

        @block.tensor
        def _(pe):
            def three(dst, a_hi, a_lo, b_hi, b_lo, first, last):
                nc.tensor.matmul(dst, a_hi, b_hi, start=first, stop=False)
                nc.tensor.matmul(dst, a_hi, b_lo, start=False, stop=False)
                return nc.tensor.matmul(dst, a_lo, b_hi, start=False, stop=last)

            def pj_free(use):
                if not isinstance(use, int) or use >= 2:
                    pe.wait_ge(pj_done, use - 1)

            def project_q(m, g, use, bank, tiles=range(KT)):
                if 0 in tiles:
                    pj_free(use)
                for c in tiles:
                    last = three(ps_pj[bank][:], w_hi[m][:, c, g * P:(g + 1) * P], w_lo[m][:, c, g * P:(g + 1) * P],
                                 xnT_hi[:, c, :], xnT_lo[:, c, :], c == 0, c == KT - 1)
                if KT - 1 in tiles:
                    last.then_inc(pj_ready, 1)

            def project_v(t, use, bank):
                pj_free(use)
                for c in range(KT):
                    last = three(ps_pj[bank][:], xnT_hi[:, c, t * P:(t + 1) * P], xnT_lo[:, c, t * P:(t + 1) * P],
                                 w_hi[2][:, c, :], w_lo[2][:, c, :], c == 0, c == KT - 1)
                last.then_inc(pj_ready, 1)

            def transpose_x(t, use, bank):
                pj_free(use)
                for c in range(KT):
                    last = nc.tensor.transpose(ps_pj[bank][:, c * P:(c + 1) * P], x_in[:, t % 2, c * P:(c + 1) * P], ident[:])
                last.then_inc(pj_ready, 1)

            def maxima_tile(g, u, n):
                j, t = u // TT, u % TT
                if not isinstance(n, int) or n >= 2:
                    pe.wait_ge(m_done, n - 1)
                nc.tensor.matmul(ps_m[u % 2][:], stacks[g][0:STACK, 0, j, t * P:(t + 1) * P], stacks[g][0:STACK, 1, j, :],
                                 start=True, stop=True).then_inc(m_ready, 1)

            def transpose_max(group):
                pe.wait_ge(m_done, UNITS * (group + 1))
                if not isinstance(group, int) or group >= 2:
                    pe.wait_ge(recip_done, group - 1)
                nc.tensor.transpose(ps_sum[0:UNITS, 0:P], neg_max_of(group), ident[:]).then_inc(maxT_ready, 1)

            def neg_max_of(group):
                return neg_max[:, GPAR[0], :]

            GPAR = [0]

            def lora(uses):
                for n in uses:
                    m, c = n // KT, n % KT
                    if n >= len(ps_lora):
                        pe.wait_ge(lora_done, n - len(ps_lora) + 1)
                    pe.wait_ge(lora_lo[m // 2], 2)
                    nc.tensor.matmul(ps_lora[n % len(ps_lora)][:], lora_stack[0:STACK, 0, m, c * P:(c + 1) * P],
                                     lora_stack[0:STACK, 1, m, :],
                                     start=True, stop=True).then_inc(lora_ready, 1)

            lora(range(0, 6))
            pe.wait_ge(consts_ready, 3)
            for t in range(TT):
                pe.wait_ge(xn_ready, t + 1)
                transpose_x(t, AT_LN + t, (AT_LN + t) % 2)
            lora(range(6, 10))
            pe.wait_ge(pj_done, AT_LN + TT)
            pe.wait_ge(w_lo_done[0], KT)
            project_q(0, 0, AT_Q[0], AT_Q[0] % 2)
            lora(range(10, 12))
            pe.wait_ge(w_lo_done[1], KT)
            project_q(1, 0, AT_Q[0] + 1, (AT_Q[0] + 1) % 2)
            pe.wait_ge(w_lo_done[2], KT)
            for t in range(TT):
                project_v(t, AT_V + t, (AT_V + t) % 2)
            lora(range(12, 16))
            pe.wait_ge(stack_loaded[0], STACK_DMAS)
            for u in range(UNITS):
                maxima_tile(0, u, u)
                if u % 2:
                    m, c = u // (2 * KT), u // 2 % KT
                    project_q(m, 1, AT_Q[1] + m, (AT_Q[1] + m) % 2, range(c, c + 1))
            pe.wait_ge(lora_done, 4 * KT)
            transpose_max(0)
            for m in range(2):
                project_q(m, 2, AT_Q[2] + m, (AT_Q[2] + m) % 2)
            pe.wait_ge(consts_ready, 3 + GROUPS)

            def body(b, first, last):
                for slot in range(GROUPS):
                    group = GROUPS * b + slot
                    nslot, nb = next_group(slot, b)
                    maxima = not (last and slot == GROUPS - 1)
                    m_next = 0
                    pe.wait_ge(row_loaded, 16 * (group + 1))
                    for u in range(UNITS):
                        kt, j = u // GH, u % GH
                        n = UNITS * group + u
                        if not (first and slot == 0 and u < 2):
                            pe.wait_ge(exp_done, n - 1)
                        s = nc.tensor.matmul(ps_s[u % 2][:], stacks[slot][0:STACK + 1, 1, j, kt * P:(kt + 1) * P],
                                             stacks[slot][0:STACK + 1, 0, j, :], start=True, stop=True)
                        s.then_inc(s_ready, 1)
                        if u in (6, 10, 14):
                            weigh(b, slot, group, (u - 6) // GH)
                        if slot == 1 and not last and u in LN_AFTER:
                            t = LN_AFTER[u]
                            pe.wait_ge(xn_ready, TT * (b + 1) + t + 1)
                            transpose_x(t, *pj(b, "ln", 0, t))
                        if maxima:
                            for _ in range(M_AFTER[u]):
                                if m_next == 0:
                                    pe.wait_ge(stack_loaded[nslot], STACK_DMAS * (nb + 1))
                                maxima_tile(nslot, m_next, UNITS * (group + 1) + m_next)
                                m_next += 1
                    project = slot == 0 or not last
                    if project:
                        if slot == 1:
                            pe.wait_ge(pj_done, pj(b, "ln", 0, TT - 1)[0] + 1)
                        project_q(0, (slot + 3) % GROUPS, *pj(b, "q", slot), range(0, 1))
                    if maxima:
                        GPAR[0] = (slot + 1) % 2
                        transpose_max(group + 1)
                    weigh(b, slot, group, KK - 1)
                    if maxima:
                        pe.wait_ge(maxT_done, group + 2)
                    else:
                        pe.wait_ge(recip_done, group)
                    pe.wait_ge(psum_added, 2 * GH * (group + 1))
                    for j in range(GH):
                        nc.tensor.matmul(ps_sum[j * HD:(j + 1) * HD, :], ones[:], p_sum[:, j, :], start=True, stop=False)
                        last_mm = nc.tensor.matmul(ps_sum[j * HD:(j + 1) * HD, :], ones[:], probs[:, (KK - 1) % 2, j, :],
                                                   start=False, stop=True)
                    last_mm.then_inc(sum_ready, 1)
                    if project:
                        project_q(0, (slot + 3) % GROUPS, *pj(b, "q", slot), range(1, KT))
                        project_q(1, (slot + 3) % GROUPS, *pj(b, "k", slot))
                    if slot == 0 and not last:
                        for t in range(2):
                            pe.wait_ge(xn_ready, TT * (b + 1) + t + 1)
                            transpose_x(t, *pj(b, "ln", 0, t))
                if not last:
                    for t in range(TT):
                        project_v(t, *pj(b, "v", 0, t))
                if first:
                    pe.wait_ge(w_lo_done[3], KT)
                pe.wait_ge(oT_lo_done, GROUPS * (b + 1))
                for t in range(TT):
                    o_use, bank = pj(b, "o", 0, t)
                    pj_free(o_use)
                    for g in range(GROUPS):
                        last_mm = three(ps_pj[bank][:], oT_hi[:, g, t * P:(t + 1) * P], oT_lo[:, g, t * P:(t + 1) * P],
                                        w_hi[3][:, g, :], w_lo[3][:, g, :], g == 0, g == GROUPS - 1)
                    last_mm.then_inc(pj_ready, 1)

            def weigh(b, slot, group, kt):
                pe.wait_ge(exp_done, UNITS * group + GH * (kt + 1))
                if kt == 0:
                    if not isinstance(group, int) or group >= 1:
                        pe.wait_ge(o_raw_done, group)
                    if slot == 0:
                        v_at = AT_V + TT - 1 if isinstance(b, int) and b == 0 else pj(b - 1, "v", 0, TT - 1)[0]
                        pe.wait_ge(pj_done, v_at + 1)
                for j in range(GH):
                    head = slot * GH + j
                    mm = nc.tensor.matmul(ps_o[j * HD:(j + 1) * HD, :], v_sb[:, kt, head * HD:(head + 1) * HD],
                                          probs[:, kt % 2, j, :], start=kt == 0, stop=kt == KK - 1)
                mm.then_inc(pv_done, 1)

            per_batch(body, pe, pe.Fori)

            def transpose_xn2(c):
                for t in range(TT):
                    if c == 0 and t == 0:
                        pe.wait_ge(pj_done, pj(LAST, "o", 0, TT - 1)[0] + 1)
                    if c >= 3:
                        pe.wait_ge(y_done, TT * (c - 3) + t + 1)
                    pe.wait_ge(xn2_ready, TT * c + t + 1)
                    for k in range(KT):
                        mm = nc.tensor.transpose(ps_y[t][:, k * P:(k + 1) * P], xn2[:, t, k * P:(k + 1) * P], ident[:])
                    mm.then_inc(xn2T_ready, 1)

            def down(q, s, c):
                if c == 0:
                    pe.wait_ge(ffw_lo, 5 * s + 5)
                pe.wait_ge(hT_lo_done, q + 1)
                pe.wait_ge(hT_hi_done, q + 1)
                for t in range(TT):
                    if not isinstance(q, int) or q >= 1:
                        pe.wait_ge(y_done, TT * (q - 1) + t + 1)
                    for j in range(J):
                        mm = three(ps_y[t][:], hT_hi[:, j, t * P:(t + 1) * P], hT_lo[:, j, t * P:(t + 1) * P],
                                   dn_hi[:, j, :], dn_lo[:, j, :], j == 0, j == J - 1)
                    mm.then_inc(down_ready, 1)

            transpose_xn2(0)

            def block_step(s, first, last):
                for c in range(BATCHES):
                    q = BATCHES * s + c
                    if first:
                        pe.wait_ge(xn2T_done, TT * (c + 1))
                    for j in range(J):
                        n = J * q + j
                        if c == 0:
                            pe.wait_ge(ffw_lo, 5 * s + j + 1)
                        for part, (dst, freed, ready) in enumerate(((ps_gate, silu_done, gate_ready), (ps_up, h_ready, up_ready))):
                            if not first or n >= 2:
                                pe.wait_ge(freed, n - 1)
                            for k in range(KT):
                                mm = three(dst[j % 2][:], gu_hi[:, j, part, k * P:(k + 1) * P], gu_lo[:, j, part, k * P:(k + 1) * P],
                                           xn2T_hi[:, k, c * L:(c + 1) * L], xn2T_lo[:, k, c * L:(c + 1) * L],
                                           k == 0, k == KT - 1)
                            mm.then_inc(ready, 1)
                        if first and j == 1 and c < BATCHES - 1:
                            transpose_xn2(c + 1)
                    if first and c >= 1:
                        pe.wait_ge(xn2T_done, min(TT * (c + 2), NT))
                    if c:
                        down(q - 1, s, c - 1)
                    elif not first:
                        down(q - 1, s - 1, BATCHES - 1)

            per_block(block_step, pe.Fori)
            down(NT - 1, SB - 1, BATCHES - 1)

        @block.gpsimd
        def _(pool):
            nc.gpsimd.memset(ident[:], 0.0).then_inc(ident_zeroed, 1)
            nc.gpsimd.memset(lora_raw[0:STACK, 1], 0.0).then_inc(lora_zeroed[1], 1)
            pool.wait_ge(lora_zeroed[1], 1)
            nc.gpsimd.memset(neg_half[:], -0.5).then_inc(consts_ready, 1)
            nc.gpsimd.memset(ones[:], 1.0).then_inc(consts_ready, 1)
            pool.wait_ge(ident_zeroed, 1)
            nc.gpsimd.affine_select(out=ident[:], in_=ident[:], compare_op=ALU.not_equal, fill=1.0, base=0,
                                    pattern=[[-1, P]], channel_multiplier=1).then_inc(consts_ready, 1)

            def inverse_deviation(n, at):
                pool.wait_ge(var_ready, n + 1)
                nc.gpsimd.tensor_tensor(rstd[:, at], var_eps[:, at], neg_half[:, at], ALU.pow).then_inc(rstd_ready, 1)

            def weight_lo(m):
                for c in range(KT):
                    pool.wait_ge(w_hi_done[m], c + 1)
                    nc.gpsimd.tensor_tensor(w_lo[m][:, c], w_raw[m][:, c], w_hi[m][:, c].bitcast(F32), ALU.subtract)\
                      .then_inc(w_lo_done[m], 1)

            for g in range(GROUPS):
                pool.wait_ge(consts_ready, 3 + g)
                nc.gpsimd.memset(stacks[g][STACK:STACK + 1, 1, :, :].bitcast(F32), 1.0).then_inc(consts_ready, 1)
            pool.wait_ge(consts_ready, 3 + GROUPS)
            inverse_deviation(0, slice(0, TT))
            pool.wait_ge(rstd_ready, 1)
            split_lora_lo(pool, nc.gpsimd, 1)
            pool.wait_ge(lora_lo[1], 2)
            weight_lo(0)
            weight_lo(2)
            weight_lo(3)

            def body(b, first, last):
                for slot in range(GROUPS):
                    group = GROUPS * b + slot
                    for kt in range(1, KK - 1):
                        if slot < 2 and not last and kt == 2:
                            inverse_deviation(2 * b + slot + 1, slice(2 * slot, 2 * slot + 2))
                        for j in range(GH):
                            pool.wait_ge(exp_done, UNITS * group + GH * kt + j + 1)
                            if kt == 1:
                                if not isinstance(group, int) or group >= 1:
                                    pool.wait_ge(sum_ready, group)
                                a = probs[:, 0, j, :]
                            else:
                                pool.wait_ge(psum_added, 2 * GH * group + GH * (kt - 2) + j + 1)
                                a = p_sum[:, j, :]
                            nc.gpsimd.tensor_tensor(p_sum[:, j, :], a, probs[:, kt % 2, j, :], ALU.add).then_inc(psum_added, 1)
                if first:
                    pool.wait_ge(bo_loaded, 16)
                pool.wait_ge(x_res_loaded, 16 * (b + 1))
                for t in range(TT):
                    nc.gpsimd.tensor_tensor(x_res[:, t, :], x_res[:, t, :], bo_sb[:], ALU.add).then_inc(x_res_ready, 1)

            per_batch(body, pool, pool.Fori)

            def split_gu(s, j):
                pool.wait_ge(ffw_hi, 5 * s + j + 1)
                nc.gpsimd.tensor_tensor(gu_lo[:, j], gu_raw[:, j], gu_hi[:, j].bitcast(F32), ALU.subtract).then_inc(ffw_lo, 1)

            def split_dn(s):
                pool.wait_ge(ffw_hi, 5 * s + 5)
                nc.gpsimd.tensor_tensor(dn_lo[:], dn_raw[:], dn_hi[:].bitcast(F32), ALU.subtract).then_inc(ffw_lo, 1)

            def pow2(c):
                pool.wait_ge(var2_ready, c + 1)
                nc.gpsimd.tensor_tensor(rstd[:, 0:TT], var_eps[:, 0:TT], neg_half[:, 0:TT], ALU.pow).then_inc(rstd2_ready, 1)

            for j in range(J):
                split_gu(0, j)
            pow2(0)
            split_dn(0)
            for c in range(1, BATCHES):
                pow2(c)

            def block_step(s, first, last):
                if not first:
                    split_dn(s)
                if not last:
                    for j in range(J):
                        split_gu(s + 1, j)

            per_block(block_step, pool.Fori)

        @block.scalar
        def _(act):
            def hi_of(dst, src, bias_col=None):
                if bias_col is None:
                    return nc.scalar.activation(dst, src, ACT.Copy)
                return nc.scalar.activation(dst, src, ACT.Identity, bias=bias_col)

            def xnT_part(t, use, bank):
                act.wait_ge(pj_ready, use + 1)
                hi_of(xnT_hi[:, :, t * P:(t + 1) * P],
                      ps_pj[bank][:].rearrange("p (c n) -> p c n", c=KT)).then_inc(xnT_hi_done, 1)

            def qk_part(m, g, use, bank, parts=qk_parts):
                act.wait_ge(pj_ready, use + 1)
                hi_of(parts[:, (Q_HI, K_HI)[m], :], ps_pj[bank][:], bias[:, m, g:g + 1]).then_inc(qk_hi_done, 1)

            def max_row(slot, group):
                act.wait_ge(maxT_ready, group + 1)
                if not isinstance(group, int) or group >= 1:
                    act.wait_ge(row_loaded, 16 * group)
                hi_of(row_max[0:UNITS, :], ps_sum[0:UNITS, 0:P]).then_inc(maxT_done, 1)
                act.wait_ge(maxT_done, group + 1)
                act.dma_start(stacks[slot][STACK:STACK + 1, 0, :, :].bitcast(F32), row_max[0:UNITS, :].bitcast(F32))\
                   .then_inc(row_loaded, 16)

            def weight_hi(m):
                for c in range(KT):
                    act.wait_ge(lora_done, KT * m + c + 1)
                    hi_of(w_hi[m][:, c], w_raw[m][:, c]).then_inc(w_hi_done[m], 1)

            act.wait_ge(lora_loaded, 16 * 6)
            for half in range(2):
                for side in range(2):
                    hi_of(lora_stack[0:STACK, side, 2 * half:2 * half + 2], lora_raw[0:STACK, side, 2 * half:2 * half + 2]).then_inc(lora_hi, 1)
            weight_hi(0)
            for t in range(TT):
                xnT_part(t, AT_LN + t, (AT_LN + t) % 2)
            weight_hi(1)
            act.wait_ge(bias_loaded, 16)
            weight_hi(2)
            qk_part(0, 0, AT_Q[0], AT_Q[0] % 2)
            qk_part(1, 0, AT_Q[0] + 1, (AT_Q[0] + 1) % 2)
            qk_part(0, 1, AT_Q[1], AT_Q[1] % 2, qk_parts1)
            qk_part(1, 1, AT_Q[1] + 1, (AT_Q[1] + 1) % 2, qk_parts1)
            max_row(0, 0)
            weight_hi(3)
            act.wait_ge(stack_loaded[0], STACK_DMAS)
            qk_part(0, 2, AT_Q[2], AT_Q[2] % 2)
            qk_part(1, 2, AT_Q[2] + 1, (AT_Q[2] + 1) % 2)

            def body(b, first, last):
                for slot in range(GROUPS):
                    group = GROUPS * b + slot
                    nslot, nb = next_group(slot, b)
                    maxima = not (last and slot == GROUPS - 1)
                    for u in range(UNITS):
                        kt, j = u // GH, u % GH
                        n = UNITS * group + u
                        act.wait_ge(s_ready, n + 1)
                        if not (first and slot == 0 and kt < 2):
                            if j == 0:
                                act.wait_ge(pv_done, KK * group + kt - 1)
                            if kt == 1:
                                if j == 0:
                                    act.wait_ge(sum_ready, group)
                            else:
                                act.wait_ge(psum_added, 2 * GH * group + (j + 1 if kt else j + 1 - GH))
                        nc.scalar.activation(probs[:, kt % 2, j, :], ps_s[u % 2][:], ACT.Exp, scale=SCALE).then_inc(exp_done, 1)
                        if slot == 1 and not last and u in LN_AFTER:
                            xnT_part(LN_AFTER[u], *pj(b, "ln", 0, LN_AFTER[u]))
                    if maxima:
                        max_row(nslot, group + 1)
                    if slot == 0 or not last:
                        prev = (slot + 2) % GROUPS
                        act.wait_ge(stack_loaded[prev], STACK_DMAS * (b + (1 if slot < 2 else 2)))
                        qk_part(0, (slot + 3) % GROUPS, *pj(b, "q", slot))
                        qk_part(1, (slot + 3) % GROUPS, *pj(b, "k", slot))
                    if slot == 0 and not last:
                        for t in range(2):
                            xnT_part(t, *pj(b, "ln", 0, t))
                    if last and slot == 2:
                        ffn_weights(0)
                act.wait_ge(o_raw_done, GROUPS * (b + 1))
                for g in range(GROUPS):
                    hi_of(oT_hi[:, g, :], o_raw[:, g, :], bias[:, 2, g:g + 1]).then_inc(oT_hi_done, 1)

            def gu_hi_part(s, j):
                act.wait_ge(gu_loaded[j], 16 * (s + 1))
                hi_of(gu_hi[:, j], gu_raw[:, j]).then_inc(ffw_hi, 1)

            def dn_hi_part(s):
                act.wait_ge(dn_loaded, 16 * (s + 1))
                hi_of(dn_hi[:], dn_raw[:]).then_inc(ffw_hi, 1)

            def ffn_weights(s):
                for j in range(J):
                    gu_hi_part(s, j)
                dn_hi_part(s)

            per_batch(body, act, act.Fori)

            def xn2T_part(c):
                for t in range(TT):
                    act.wait_ge(xn2T_ready, TT * c + t + 1)
                    hi_of(xn2T_hi[:, :, c * L + t * P:c * L + (t + 1) * P],
                          ps_y[t][:].rearrange("p (c n) -> p c n", c=KT)).then_inc(xn2T_hi_done, 1)

            xn2T_part(0)

            def block_step(s, first, last):
                for c in range(BATCHES):
                    q = BATCHES * s + c

                    def gate(j):
                        n = J * q + j
                        act.wait_ge(gate_ready, n + 1)
                        if not first or n >= 2:
                            act.wait_ge(h_ready, n - 1)
                        nc.scalar.activation(silu[:, j % 2, :], ps_gate[j % 2][:], ACT.Silu).then_inc(silu_done, 1)

                    def size(j):
                        act.wait_ge(h_ready, J * q + j + 1)
                        if not first or c >= 1:
                            act.wait_ge(mask_step, 10 * (q - 1) + 3)
                        nc.scalar.activation(h_abs[:, j, :], h[:, j, :], ACT.Abs).then_inc(abs_done, 1)

                    gate(0)
                    gate(1)
                    if c == 1 and not first:
                        dn_hi_part(s)
                    size(0)
                    if first and c < BATCHES - 1:
                        xn2T_part(c + 1)
                    gate(2)
                    size(1)
                    gate(3)
                    size(2)
                    if c == BATCHES - 1 and not last:
                        gu_hi_part(s + 1, 0)
                        gu_hi_part(s + 1, 1)
                    size(3)
                    if c == BATCHES - 1 and not last:
                        gu_hi_part(s + 1, 2)
                        gu_hi_part(s + 1, 3)
                    if not first or c >= 1:
                        act.wait_ge(down_ready, TT * q)
                    act.wait_ge(h_kept, J * (q + 1))
                    hi_of(hT_hi[:], h[:]).then_inc(hT_hi_done, 1)

            per_block(block_step, act.Fori)

        @block.vector
        def _(dve):
            def statistics(src, step, var_sem, loaded, count, tiles=range(TT), arrived=16):
                n = len(tiles)
                dve.wait_ge(loaded, arrived)
                for t in tiles:
                    nc.vector.bn_stats(stats[:, t, :], src(t)).then_inc(step, 1)
                for i, t in enumerate(tiles):
                    dve.wait_ge(step, count + i + 1)
                    nc.vector.bn_aggr(mv[:, t, :], stats[:, t, :]).then_inc(step, 1)
                dve.wait_ge(step, count + 2 * n)
                at = slice(tiles[0], tiles[0] + n)
                nc.vector.tensor_scalar(var_eps[:, at], mv[:, at, 1], EPS, None, ALU.add).then_inc(var_sem, 1)

            def normalise(dst, src, mean, r):
                return nc.vector.tensor_scalar(dst, src, mean, r, ALU.subtract, ALU.mult)

            def xnT_part(t, use, bank, n):
                dve.wait_ge(xnT_hi_done, n + 1)
                nc.vector.tensor_tensor(xnT_lo[:, :, t * P:(t + 1) * P],
                                        ps_pj[bank][:].rearrange("p (c n) -> p c n", c=KT),
                                        xnT_hi[:, :, t * P:(t + 1) * P].bitcast(F32), ALU.subtract).then_inc(pj_done, 1)

            def qk_part(m, g, bank, n, parts=qk_parts):
                dve.wait_ge(qk_hi_done, n + 1)
                nc.vector.scalar_tensor_tensor(parts[:, (Q_LO, K_LO)[m], :], ps_pj[bank][:], bias[:, m, g:g + 1],
                                               parts[:, (Q_HI, K_HI)[m], :].bitcast(F32), ALU.add, ALU.subtract).then_inc(pj_done, 1)

            def v_part(t, use, bank):
                dve.wait_ge(pj_ready, use + 1)
                nc.vector.tensor_copy(v_sb[:, t, :], ps_pj[bank][:]).then_inc(pj_done, 1)

            def reduce(u, n, par):
                dve.wait_ge(m_ready, n + 1)
                nc.vector.tensor_reduce(neg_max[:, par, u:u + 1], ps_m[u % 2][:], AX.X, ALU.max, negate=True).then_inc(m_done, 1)

            def lora_part(m):
                dve.wait_ge(w_loaded[m], 16)
                for c in range(KT):
                    n = KT * m + c
                    dve.wait_ge(lora_ready, n + 1)
                    nc.vector.scalar_tensor_tensor(w_raw[m][:, c, :], ps_lora[n % len(ps_lora)][:], LORA, w_raw[m][:, c, :],
                                                   ALU.mult, ALU.add).then_inc(lora_done, 1)

            nc.vector.memset(lora_raw[0:STACK, 0], 0.0).then_inc(lora_zeroed[0], 1)
            statistics(lambda t: x_first[:, t, :], stats_step, var_ready, x_first_loaded, 0)
            split_lora_lo(dve, nc.vector, 0)
            lora_part(0)
            dve.wait_ge(rstd_ready, 1)
            for t in range(2):
                normalise(x_in[:, t, :], x_first[:, t, :], mv[:, t, 0:1], rstd[:, t:t + 1]).then_inc(xn_ready, 1)
            for t in range(TT):
                xnT_part(t, AT_LN + t, (AT_LN + t) % 2, t)
                if t < 2:
                    normalise(x_in[:, t, :], x_first[:, t + 2, :], mv[:, t + 2, 0:1], rstd[:, t + 2:t + 3]).then_inc(xn_ready, 1)
            lora_part(1)
            for c in range(KT):
                dve.wait_ge(w_hi_done[1], c + 1)
                nc.vector.tensor_tensor(w_lo[1][:, c], w_raw[1][:, c], w_hi[1][:, c].bitcast(F32), ALU.subtract)\
                  .then_inc(w_lo_done[1], 1)
            dve.wait_ge(bias_loaded, 16)
            lora_part(2)
            qk_part(0, 0, AT_Q[0] % 2, 0)
            qk_part(1, 0, (AT_Q[0] + 1) % 2, 1)
            for t in range(TT):
                v_part(t, AT_V + t, (AT_V + t) % 2)
            lora_part(3)
            for u in range(UNITS):
                reduce(u, u, 0)
                if u == 9:
                    qk_part(0, 1, AT_Q[1] % 2, 2, qk_parts1)
            qk_part(1, 1, (AT_Q[1] + 1) % 2, 3, qk_parts1)
            qk_part(0, 2, AT_Q[2] % 2, 4)
            qk_part(1, 2, (AT_Q[2] + 1) % 2, 5)

            def body(b, first, last):
                for slot in range(GROUPS):
                    group = GROUPS * b + slot
                    maxima = not (last and slot == GROUPS - 1)
                    m_next = 0
                    for u in range(UNITS):
                        if slot == 1 and not last and u in LN_AFTER:
                            t = LN_AFTER[u]
                            ln_use, bank = pj(b, "ln", 0, t)
                            xnT_part(t, ln_use, bank, TT * (b + 1) + t)
                        if slot < 2 and not last and u - 1 in STATS_AFTER[slot][:2]:
                            dve.wait_ge(stats_step, 2 * TT * (b + 1) + TT * slot + 2 * (u - STATS_AFTER[slot][0]))
                        if maxima:
                            for _ in range(M_AFTER[u]):
                                reduce(m_next, UNITS * (group + 1) + m_next, (slot + 1) % 2)
                                m_next += 1
                        if slot < 2 and not last and u in STATS_AFTER[slot]:
                            next_statistics(b, slot, STATS_AFTER[slot].index(u))
                        if slot < 2 and not last and u == NORMALISE_AFTER[slot]:
                            next_normalise(b, slot)
                    dve.wait_ge(sum_ready, group + 1)
                    nc.vector.reciprocal(recip[:], ps_sum[:]).then_inc(recip_done, 1)
                    dve.wait_ge(recip_done, group + 1)
                    if slot == 0 and not first:
                        dve.wait_ge(oT_hi_done, GROUPS * b)
                    nc.vector.tensor_tensor(o_raw[:, slot, :], ps_o[:], recip[:], ALU.mult).then_inc(o_raw_done, 1)
                    if slot == 0 or not last:
                        for m, what in enumerate("qk"):
                            qk_part(m, (slot + 3) % GROUPS, pj(b, what, slot)[1], 6 + 8 * b + 2 * slot + m)
                    if slot == 0 and not last:
                        for t in range(2):
                            xnT_part(t, *pj(b, "ln", 0, t), TT * (b + 1) + t)
                for g in range(GROUPS):
                    if not last and g < 3:
                        v_part(g, *pj(b, "v", 0, g))
                    dve.wait_ge(oT_hi_done, GROUPS * b + g + 1)
                    nc.vector.scalar_tensor_tensor(oT_lo[:, g, :], o_raw[:, g, :], bias[:, 2, g:g + 1],
                                                   oT_hi[:, g, :].bitcast(F32), ALU.add, ALU.subtract).then_inc(oT_lo_done, 1)
                if not last:
                    v_part(3, *pj(b, "v", 0, 3))
                for t in range(TT):
                    o_use, bank = pj(b, "o", 0, t)
                    dve.wait_ge(pj_ready, o_use + 1)
                    dve.wait_ge(x_res_ready, TT * b + t + 1)
                    nc.vector.tensor_tensor(x_res[:, t, :], ps_pj[bank][:], x_res[:, t, :], ALU.add).then_inc(pj_done, 1)

            def next_statistics(b, pair, step):
                tiles = range(2 * pair, 2 * pair + 2)
                if step == 0:
                    for t in tiles:
                        dve.wait_ge(x_in_loaded[t % 2], 32 * b + 16 * (pair + 1))
                        nc.vector.bn_stats(stats[:, t, :], x_in[:, t % 2, :]).then_inc(stats_step, 1)
                elif step == 1:
                    for t in tiles:
                        nc.vector.bn_aggr(mv[:, t, :], stats[:, t, :]).then_inc(stats_step, 1)
                else:
                    nc.vector.tensor_scalar(var_eps[:, tiles[0]:tiles[0] + 2], mv[:, tiles[0]:tiles[0] + 2, 1], EPS, None,
                                            ALU.add).then_inc(var_ready, 1)

            def next_normalise(b, pair):
                dve.wait_ge(rstd_ready, 2 * b + pair + 2)
                for t in range(2 * pair, 2 * pair + 2):
                    normalise(x_in[:, t % 2, :], x_in[:, t % 2, :], mv[:, t, 0:1], rstd[:, t:t + 1]).then_inc(xn_ready, 1)

            per_batch(body, dve, dve.Fori)

            def norm2(c):
                statistics(lambda t: y[:, c * TT + t, :], stats2_step, var2_ready,
                           x2_back[c] if c < LAST else pj_done, 2 * TT * c,
                           arrived=16 if c < LAST else pj(LAST, "o", 0, TT - 1)[0] + 1)
                dve.wait_ge(rstd2_ready, c + 1)
                for t in range(TT):
                    if c:
                        dve.wait_ge(xn2T_ready, TT * (c - 1) + t + 1)
                    normalise(xn2[:, t, :], y[:, c * TT + t, :], mv[:, t, 0:1], rstd[:, t:t + 1]).then_inc(xn2_ready, 1)

            def xn2T_part(c):
                for t in range(TT):
                    dve.wait_ge(xn2T_hi_done, TT * c + t + 1)
                    at = slice(c * L + t * P, c * L + (t + 1) * P)
                    nc.vector.tensor_tensor(xn2T_lo[:, :, at], ps_y[t][:].rearrange("p (c n) -> p c n", c=KT),
                                            xn2T_hi[:, :, at].bitcast(F32), ALU.subtract).then_inc(xn2T_done, 1)

            norm2(0)
            xn2T_part(0)

            def add_down(q, c):
                for t in range(TT):
                    dve.wait_ge(down_ready, TT * q + t + 1)
                    nc.vector.tensor_tensor(y[:, c * TT + t, :], ps_y[t][:], y[:, c * TT + t, :], ALU.add).then_inc(y_done, 1)

            def block_step(s, first, last):
                for c in range(BATCHES):
                    q = BATCHES * s + c
                    if first and c < BATCHES - 1:
                        norm2(c + 1)
                    for j in range(J):
                        n = J * q + j
                        dve.wait_ge(up_ready, n + 1)
                        dve.wait_ge(silu_done, n + 1)
                        if j == 0 and not (first and c == 0):
                            dve.wait_ge(hT_hi_done, q)
                            dve.wait_ge(hT_lo_done, q)
                        nc.vector.tensor_tensor(h[:, j, :], ps_up[j % 2][:], silu[:, j % 2, :], ALU.mult).then_inc(h_ready, 1)
                        if first and j == 1 and c < BATCHES - 1:
                            xn2T_part(c + 1)
                    step = 10 * q
                    dve.wait_ge(abs_done, J * (q + 1))
                    nc.vector.tensor_tensor(pair_max[:], h_abs[:, 0:J:2, :], h_abs[:, 1:J:2, :], ALU.max).then_inc(mask_step, 1)
                    nc.vector.tensor_tensor(pair_min[:], h_abs[:, 0:J:2, :], h_abs[:, 1:J:2, :], ALU.min).then_inc(mask_step, 1)
                    nc.vector.tensor_tensor(first_wins[:], h_abs[:, 0:J:2, :], h_abs[:, 1:J:2, :], ALU.is_ge).then_inc(mask_step, 1)
                    dve.wait_ge(mask_step, step + 2)
                    nc.vector.tensor_tensor(both_01[:], pair_min[:, 0, :], pair_max[:, 1, :], ALU.is_ge).then_inc(mask_step, 1)
                    nc.vector.tensor_tensor(both_23[:], pair_min[:, 1, :], pair_max[:, 0, :], ALU.is_gt).then_inc(mask_step, 1)
                    dve.wait_ge(mask_step, step + 5)
                    nc.vector.tensor_tensor(tilt[:], both_01[:], both_23[:], ALU.subtract).then_inc(mask_step, 1)
                    dve.wait_ge(mask_step, step + 6)
                    for i in range(2):
                        nc.vector.tensor_tensor(wins_up[:, i, :], first_wins[:, i, :], tilt[:], ALU.add).then_inc(mask_step, 1)
                        nc.vector.tensor_tensor(wins_down[:, i, :], first_wins[:, i, :], tilt[:], ALU.subtract).then_inc(mask_step, 1)
                    dve.wait_ge(mask_step, step + 10)
                    kept = ((wins_up, 0, ALU.is_ge, 1.0), (wins_down, 0, ALU.is_le, 0.0),
                            (wins_down, 1, ALU.is_ge, 1.0), (wins_up, 1, ALU.is_le, 0.0))
                    for j, (wins, i, op, bound) in enumerate(kept):
                        nc.vector.scalar_tensor_tensor(h[:, j, :], wins[:, i, :], bound, h[:, j, :], op, ALU.mult).then_inc(h_kept, 1)
                    dve.wait_ge(hT_hi_done, q + 1)
                    nc.vector.tensor_tensor(hT_lo[:], h[:], hT_hi[:].bitcast(F32), ALU.subtract).then_inc(hT_lo_done, 1)
                    if c:
                        add_down(q - 1, c - 1)
                    elif not first:
                        add_down(q - 1, BATCHES - 1)

            per_block(block_step, dve.Fori)
            add_down(NT - 1, BATCHES - 1)


def kernel(**inputs):
    import numpy as np
    import concourse.bacc as bacc
    from concourse.bass_utils import run_bass_kernel_spmd

    a = {k.replace("L0_attn_", "").replace("L0_ffn_", ""): np.asarray(v) for k, v in inputs.items()}
    names = "qkvo"
    arrays = {
        "x_in": a["x"].reshape(NT, P, D).transpose(1, 0, 2),
        "wqkvo_in": np.stack([a["W" + n].T.reshape(KT, P, D).transpose(1, 0, 2) for n in names]),
        "lora_b_in": np.stack([a["B" + n] for n in names], axis=1),
        "lora_a_in": np.stack([a["A" + n].T for n in names], axis=1),
        "bias_cols_in": np.stack([a["b" + n].reshape(KT, P).T for n in "qkv"], axis=1),
        "bo_rows_in": np.broadcast_to(a["bo"], (P, D)),
        "w_gu_in": np.stack([a["w_" + n].reshape(KT, P, SB, P, J).transpose(1, 2, 4, 0, 3) for n in ("gate", "up")], axis=3)
                     .reshape(P, SB, J, 2, KT * P),
        "w_down_in": a["w_down"].reshape(SB, P, J, D).transpose(1, 0, 2, 3),
    }
    arrays = {k: np.ascontiguousarray(v) for k, v in arrays.items()}
    nc = bacc.Bacc("TRN2", target_bir_lowering=False, num_devices=1)
    args = [nc.dram_tensor(k, v.shape, mybir.dt.from_np(v.dtype), kind="ExternalInput").ap() for k, v in arrays.items()]
    out = nc.dram_tensor("x_out", (P, NT, D), F32, kind="ExternalOutput").ap()
    block_kernel(nc, *args, out)
    r = run_bass_kernel_spmd(nc, [arrays], core_ids=[0])
    got = r.results[0]["x_out"]
    return np.ascontiguousarray(got.transpose(1, 0, 2)).reshape(BATCHES, L, D)
```

```python
from contextlib import ExitStack

import concourse.bass as bass
import concourse.mybir as mybir

P = 128
F32 = mybir.dt.float32
F32R = mybir.dt.float32r
BF16 = mybir.dt.bfloat16
ALU = mybir.AluOpType
ACT = mybir.ActivationFunctionType
AX = mybir.AxisListType

BATCHES, L, D = 4, 512, 512
HEADS, HD, RANK = 16, 32, 16
FF = 2048
KT = D // P
TT = L // P
KK = L // P
GH = P // HD
GROUPS = HEADS // GH
NT = BATCHES * TT
J = 4
SB = FF // (J * P)
LORA = 8.0 / RANK
SCALE = HD ** -0.5
EPS = 1e-5
STACK = 3 * HD
UNITS = KK * GH
LAST = BATCHES - 1

PJ_LN, PJ_V, PJ_O = TT, TT, TT
AT_LN = 0
AT_Q0 = AT_LN + PJ_LN
AT_V = AT_Q0 + 4
AT_Q = (AT_Q0, AT_Q0 + 2, AT_V + PJ_V - 1)
PJ_START = AT_Q[2] + 3
PJ_BODY = 2 * GROUPS + PJ_LN + PJ_V + PJ_O
STACK_DMAS = 16 * 3 * GH

M_AFTER = [1] * 16
LN_AFTER = {12: 2, 13: 3}
LN_STEPS = ({5: 0, 6: 1, 7: 2, 8: 3, 12: 4, 13: 5}, {3: 0, 5: 1, 6: 2, 7: 3, 10: 4, 11: 5})
STATS2_AFTER, NORMALISE2_AFTER, LN2_AFTER = {2: 0, 5: 1}, {8: 0, 10: 1}, {10: 0, 11: 1, 13: 2, 14: 3}

FFN_LOADS = {1: ((0, "g0"), (6, "y0")), 2: ((0, "g2"), (6, "y1")), 3: ((0, "y2"), (4, "d"))}

PROJECT_AFTER, K_BEFORE = (1, 4, 8, 12), 1


def pj_use(what, slot=0):
    if what in ("q", "k"):
        return (0, 6, 8, 10)[slot] + (what == "k")
    return {"ln": 2, "v": 12, "o": 16}[what]


def block_kernel(nc, x, wqkvo, lora_b, lora_a, bias_cols, bo_rows, w_gu, w_down, out):
    x2_dram = nc.dram_tensor("x2_dram", [NT, P, D], F32, kind="Internal").ap()
    x2_flat = x2_dram.rearrange("t p d -> (t p d)")
    x_rows = x.rearrange("p t d -> p (t d)")
    w_gu_rows = w_gu.rearrange("p s j a n -> p (s j a n)")
    w_down_rows = w_down.rearrange("p s j d -> p (s j d)")
    start = -(-nc.sbuf_base // 64) * 64

    with ExitStack() as ctx:
        def sb(name, at_kb, shape, dt=F32):
            return nc.alloc_sbuf_tensor_at(name, [P] + shape, dt, offset=start + int(at_kb * 1024))

        def sem(name):
            return ctx.enter_context(nc.semaphore(name))

        w_hi = [sb(f"w_hi_{n}", 16 * i, [KT, D], F32R) for i, n in enumerate("qkvo")]
        w_lo = [sb(f"w_lo_{n}", 16 * i + 8, [KT, D], F32R) for i, n in enumerate("qkvo")]
        w_raw = [sb(f"w_raw_{n}", 16 * i + 8, [KT, D]) for i, n in enumerate("qkvo")]
        xnT_hi = sb("xnT_hi", 64, [KT, L], F32R)
        xnT_lo = sb("xnT_lo", 72, [KT, L], F32R)
        qk_parts = sb("qk_parts", 80, [4, L], F32R)
        Q_HI, Q_LO, K_LO, K_HI = range(4)
        qk_parts1 = sb("qk_parts1", 128, [4, L], F32R)
        x_in = sb("x_in", 88, [2, D])
        y = sb("y", 64, [NT, D])
        x_res = y[:, LAST * TT:, :]
        probs = sb("probs", 96, [2, GH, L])
        oT_hi = sb("oT_hi", 96, [GROUPS, L], F32R)
        oT_lo = sb("oT_lo", 104, [GROUPS, L], F32R)
        x_first = sb("x_first", 96, [TT, D])
        p_sum = sb("p_sum", 112, [GH, L])
        v_sb = sb("v_sb", 120, [KK, D])
        o_raw = sb("o_raw", 128, [GROUPS, L])
        recip = sb("recip", 136, [L])
        bo_sb = sb("bo_sb", 138, [D])
        stacks = [sb(f"stack{g}", 140 + 16 * g, [2, GH, L], F32R) for g in range(GROUPS)]
        lora_stack = sb("lora_stack", 172, [2, 4, D], F32R)
        lora_raw = sb("lora_raw", 188, [2, 4, D])
        ident = sb("ident", 204, [P])
        row_max = sb("row_max", 204.5, [P], F32R)
        stats = sb("stats", 205, [4, 6])
        mv = sb("mv", 205.25, [TT, 2])
        rstd = sb("rstd", 205.5, [TT])
        neg_half = sb("neg_half", 205.75, [TT])
        var_eps = sb("var_eps", 206, [TT])
        neg_max = sb("neg_max", 206.25, [2, UNITS])
        bias = sb("bias", 206.5, [3, KT])
        ones = sb("ones", 206.75, [HD])

        gu_hi = sb("gu_hi", 0, [J, 2, KT * P], F32R)
        gu_lo = sb("gu_lo", 16, [J, 2, KT * P], F32R)
        gu_raw = sb("gu_raw", 16, [J, 2, KT * P])
        dn_hi = sb("dn_hi", 32, [J, D], F32R)
        dn_lo = sb("dn_lo", 40, [J, D], F32R)
        dn_raw = sb("dn_raw", 40, [J, D])
        h = sb("h", 132, [J, L])
        h_abs = sb("h_abs", 56, [J, L])
        hT_hi = sb("hT_hi", 96, [J, L], F32R)
        hT_lo = sb("hT_lo", 104, [J, L], F32R)
        silu = sb("silu", 112, [2, L])
        pair_max = sb("pair_max", 116, [2, L])
        pair_min = sb("pair_min", 120, [2, L])
        first_wins = sb("first_wins", 124, [2, L], BF16)
        both_01 = sb("both_01", 126, [L], BF16)
        both_23 = sb("both_23", 127, [L], BF16)
        tilt = sb("tilt", 130, [L], BF16)
        wins_up = sb("wins_up", 126, [2, L], BF16)
        wins_down = sb("wins_down", 128, [2, L], BF16)
        xn2 = [sb(f"xn2_{c}", at, [TT, D]) for c, at in enumerate((156, 172, 188, 48))]
        xn2T_hi = [sb(f"xn2T_hi{c}", 140 + 16 * c, [KT, L], F32R) for c in range(BATCHES)]
        xn2T_lo = [sb(f"xn2T_lo{c}", 148 + 16 * c, [KT, L], F32R) for c in range(BATCHES)]

        banks = [ctx.enter_context(nc.psum_tensor(f"bank{i}", [P, 512], F32)) for i in range(8)]
        ps_s, ps_m, ps_pj, ps_o, ps_sum = banks[0:2], banks[2:4], banks[4:6], banks[6], banks[7]
        ps_lora = [banks[i] for i in (0, 1, 6, 7, 2, 3)]
        ps_gate, ps_up, ps_y = (banks[2], banks[0]), (banks[3], banks[1]), banks[4:8]

        w_loaded = [sem(f"w_loaded_{n}") for n in "qkvo"]
        x_first_loaded = sem("x_first_loaded")
        lora_loaded, bias_loaded, bo_loaded = sem("lora_loaded"), sem("bias_loaded"), sem("bo_loaded")
        consts_ready, ident_zeroed = sem("consts_ready"), sem("ident_zeroed")
        lora_ready, lora_done = sem("lora_ready"), sem("lora_done")
        lora_zeroed = [sem(f"lora_zeroed{side}") for side in range(2)]
        lora_hi, lora_lo = sem("lora_hi"), [sem(f"lora_lo{half}") for half in range(2)]
        stats_step, var_ready, rstd_ready = sem("stats_step"), sem("var_ready"), sem("rstd_ready")
        w_hi_done, w_lo_done = [[sem(f"w_{part}_done_{n}") for n in "qkvo"] for part in ("hi", "lo")]
        x_in_loaded = [sem(f"x_in_loaded{i}") for i in range(2)]
        xn_ready = sem("xn_ready")
        pj_ready, pj_done = sem("pj_ready"), sem("pj_done")
        xnT_hi_done, qk_hi_done = sem("xnT_hi_done"), sem("qk_hi_done")
        stack_loaded = [sem(f"stack_loaded{g}") for g in range(GROUPS)]
        row_loaded = sem("row_loaded")
        m_ready, m_done = sem("m_ready"), sem("m_done")
        maxT_ready, maxT_done = sem("maxT_ready"), sem("maxT_done")
        s_ready, exp_done = sem("s_ready"), sem("exp_done")
        pv_done, psum_added = sem("pv_done"), sem("psum_added")
        sum_ready, recip_done, o_raw_done = sem("sum_ready"), sem("recip_done"), sem("o_raw_done")
        oT_hi_done, oT_lo_done = sem("oT_hi_done"), sem("oT_lo_done")
        x_res_loaded = sem("x_res_loaded")
        x_res_ready = sem("x_res_ready")
        x2_stored = [sem(f"x2_stored{i}") for i in range(2)]

        gu_loaded = [sem(f"gu_loaded{j}") for j in range(J)]
        dn_loaded = sem("dn_loaded")
        ffw_hi, ffw_lo = sem("ffw_hi"), sem("ffw_lo")
        x2_back = [sem(f"x2_back{c}") for c in range(LAST)]
        stats2_step, var2_ready, rstd2_ready = sem("stats2_step"), sem("var2_ready"), sem("rstd2_ready")
        xn2_ready, xn2T_hi_done = sem("xn2_ready"), sem("xn2T_hi_done")
        gate_ready, up_ready = sem("gate_ready"), sem("up_ready")
        silu_done, h_ready, abs_done = sem("silu_done"), sem("h_ready"), sem("abs_done")
        mask_step, h_kept = sem("mask_step"), sem("h_kept")
        hT_hi_done, hT_lo_done = sem("hT_hi_done"), sem("hT_lo_done")
        down_ready, y_done = sem("down_ready"), sem("y_done")
        out_stored = sem("out_stored")

        def per_batch(body, eng, loop):
            body(0, True, False)
            with loop(1, LAST) as b:
                body(b, False, False)
            body(LAST, False, True)

        def per_block(step, loop):
            step(0, True, False)
            with loop(1, SB - 1) as s:
                step(s, False, False)
            step(SB - 1, False, True)

        def split_lora_lo(eng, ops, half):
            for side, copy in enumerate((2, 1)):
                eng.wait_ge(lora_hi, 2 * half + side + 1)
                rows, ms = slice(copy * HD, (copy + 1) * HD), slice(2 * half, 2 * half + 2)
                ops.tensor_tensor(lora_stack[rows, side, ms], lora_raw[rows, side, ms],
                                  lora_stack[rows, side, ms].bitcast(F32), ALU.subtract).then_inc(lora_lo[half], 1)

        def next_group(slot, b):
            return (slot + 1, b) if slot < GROUPS - 1 else (0, b + 1)

        def pj(b, what, slot=0, t=0):
            n = pj_use(what, slot) if what != "ln2" else 2 + TT * slot + (TT if slot == LAST else 0)
            if isinstance(b, int) and b == LAST and what == "o":
                n = 2 + TT * LAST
            return PJ_START + PJ_BODY * b + n + t, (n + t) % 2

        block = ctx.enter_context(nc.Block())

        @block.sync
        def _(sp):
            sp.dma_start(x_first[:], x[:, 0:TT, :]).then_inc(x_first_loaded, 16)
            for side in range(2):
                sp.wait_ge(lora_zeroed[side], 1)
            for copy in range(3):
                for side, factor in enumerate((lora_b, lora_a)):
                    sp.dma_start(lora_raw[copy * HD:copy * HD + RANK, side], factor).then_inc(lora_loaded, 16)
            for m in range(4):
                sp.dma_start(w_raw[m][:], wqkvo[m]).then_inc(w_loaded[m], 16)
                if m == 0:
                    sp.dma_start(bias[:], bias_cols).then_inc(bias_loaded, 16)
            sp.dma_start(bo_sb[:], bo_rows).then_inc(bo_loaded, 16)

            def held(value):
                return value if isinstance(value, int) else sp.snap(value)

            def stack(g, split, parts=qk_parts):
                sp.wait_ge(pj_done, split)
                for j in range(GH):
                    for row, (of_q, of_k) in enumerate(((Q_HI, K_HI), (Q_HI, K_LO), (Q_LO, K_HI))):
                        sp.dma_start(stacks[g][row * HD:(row + 1) * HD, :, j, :].bitcast(F32),
                                     parts[j * HD:(j + 1) * HD, of_q:of_k + 1:of_k - of_q, :].bitcast(F32))\
                          .then_inc(stack_loaded[g], 16)

            def load_x_in(b, t, transposed):
                at = held(((b + 1) * TT + t) * D)
                sp.wait_ge(pj_ready, transposed)
                sp.dma_start(x_in[:, t % 2, :], x_rows[:, bass.ds(at, D)]).then_inc(x_in_loaded[t % 2], 16)

            for g in range(3):
                if g == 1:
                    for t in range(2):
                        load_x_in(0, t, AT_LN + TT)
                if g == 2:
                    sp.wait_ge(lora_ready, 4 * KT)
                stack(g, AT_Q[g] + 2, qk_parts1 if g == 1 else qk_parts)

            def body(b, first, last):
                for slot in range(GROUPS):
                    if not last and slot == 0:
                        if not first:
                            sp.wait_ge(x2_stored[0], held(16 * b))
                        for t in range(2 if first else 0, TT):
                            load_x_in(b, t, held(pj(b, "ln", 0, t - 2)[0] + 1) if t >= 2 else
                                      held(pj(b - 1, "ln", 0, t + 2)[0] + 1))
                    if slot == (0 if last else 3):
                        transposed = held(pj(b - last, "ln", 0, TT - 1)[0] + 1)
                        at, stored = held(b * TT * D), held(16 * b)
                        sp.wait_ge(pj_ready, transposed)
                        if not first:
                            for i in range(2):
                                sp.wait_ge(x2_stored[i], stored)
                        sp.dma_start(x_res.rearrange("p t d -> p (t d)"), x_rows[:, bass.ds(at, TT * D)]).then_inc(x_res_loaded, 16)
                    if slot == 0 or not last:
                        stack((slot + 3) % GROUPS, held(pj(b, "k", slot)[0] + 1))
                    if last and slot == 1:
                        sp.wait_ge(pj_ready, pj(b, "k", 0)[0] + 1)
                        sp.wait_ge(stack_loaded[3], STACK_DMAS * BATCHES)
                    if last and slot:
                        for u, load in FFN_LOADS[slot]:
                            sp.wait_ge(s_ready, UNITS * (GROUPS * LAST + slot) + u + 1)
                            if load[0] == "y":
                                c = int(load[1])
                                sp.dma_start(y[:, c * TT:(c + 1) * TT, :],
                                             x2_dram[c * TT:(c + 1) * TT].rearrange("t p d -> p t d")).then_inc(x2_back[c], 16)
                            elif load[0] == "g":
                                for j in (int(load[1]), int(load[1]) + 1):
                                    sp.dma_start(gu_raw[:, j], w_gu[:, 0, j]).then_inc(gu_loaded[j], 16)
                            else:
                                sp.dma_start(dn_raw[:], w_down[:, 0]).then_inc(dn_loaded, 16)
                if not last:
                    for i in range(2):
                        computed, at = held(pj(b, "o", 0, 2 * i + 1)[0] + 1), held((b * TT + 2 * i) * P * D)
                        sp.wait_ge(pj_done, computed)
                        sp.dma_start(x2_flat[bass.ds(at, 2 * P * D)].rearrange("(t p d) -> p t d", t=2, p=P),
                                     x_res[:, 2 * i:2 * i + 2, :]).then_inc(x2_stored[i], 16)

            per_batch(body, sp, sp.Fori)

            def block_step(s, first, last):
                if not first:
                    done, at = held(16 * s), held(s * J * D)
                    sp.wait_ge(down_ready, done)
                    sp.dma_start(dn_raw[:].rearrange("p j d -> p (j d)"), w_down_rows[:, bass.ds(at, J * D)]).then_inc(dn_loaded, 16)
                if not last:
                    for j in range(J):
                        done, at = held(16 * s + 12 + j + 1), held(((s + 1) * J + j) * 2 * KT * P)
                        sp.wait_ge(up_ready, done)
                        sp.dma_start(gu_raw[:, j].rearrange("p a n -> p (a n)"), w_gu_rows[:, bass.ds(at, 2 * KT * P)]).then_inc(gu_loaded[j], 16)

            per_block(block_step, sp.Fori)
            for c in range(BATCHES):
                for tiles in (range(TT),) if c < LAST else [range(t, t + 1) for t in range(TT)]:
                    sp.wait_ge(y_done, NT * (SB - 1) + TT * c + tiles[-1] + 1)
                    at = slice(c * TT + tiles[0], c * TT + tiles[-1] + 1)
                    sp.dma_start(out[:, at, :], y[:, at, :]).then_inc(out_stored, 16)
            sp.wait_ge(out_stored, 16 * (LAST + TT))

        @block.tensor
        def _(pe):
            def three(dst, a_hi, a_lo, b_hi, b_lo, first, last):
                nc.tensor.matmul(dst, a_hi, b_hi, start=first, stop=False)
                nc.tensor.matmul(dst, a_hi, b_lo, start=False, stop=False)
                return nc.tensor.matmul(dst, a_lo, b_hi, start=False, stop=last)

            def pj_free(use):
                if not isinstance(use, int) or use >= 2:
                    pe.wait_ge(pj_done, use - 1)

            def project_q(m, g, use, bank, tiles=range(KT)):
                if 0 in tiles:
                    pj_free(use)
                for c in tiles:
                    last = three(ps_pj[bank][:], w_hi[m][:, c, g * P:(g + 1) * P], w_lo[m][:, c, g * P:(g + 1) * P],
                                 xnT_hi[:, c, :], xnT_lo[:, c, :], c == 0, c == KT - 1)
                if KT - 1 in tiles:
                    last.then_inc(pj_ready, 1)

            def project_v(t, use, bank):
                pj_free(use)
                for c in range(KT):
                    last = three(ps_pj[bank][:], xnT_hi[:, c, t * P:(t + 1) * P], xnT_lo[:, c, t * P:(t + 1) * P],
                                 w_hi[2][:, c, :], w_lo[2][:, c, :], c == 0, c == KT - 1)
                last.then_inc(pj_ready, 1)

            def transpose_x(t, use, bank):
                pj_free(use)
                for c in range(KT):
                    last = nc.tensor.transpose(ps_pj[bank][:, c * P:(c + 1) * P], x_in[:, t % 2, c * P:(c + 1) * P], ident[:])
                last.then_inc(pj_ready, 1)

            def maxima_tile(g, u, n):
                j, t = u // TT, u % TT
                if not isinstance(n, int) or n >= 2:
                    pe.wait_ge(m_done, n - 1)
                nc.tensor.matmul(ps_m[u % 2][:], stacks[g][0:STACK, 0, j, t * P:(t + 1) * P], stacks[g][0:STACK, 1, j, :],
                                 start=True, stop=True).then_inc(m_ready, 1)

            def transpose_max(group):
                pe.wait_ge(m_done, UNITS * (group + 1))
                if not isinstance(group, int) or group >= 2:
                    pe.wait_ge(recip_done, group - 1)
                nc.tensor.transpose(ps_sum[0:UNITS, 0:P], neg_max_of(group), ident[:]).then_inc(maxT_ready, 1)

            def neg_max_of(group):
                return neg_max[:, GPAR[0], :]

            GPAR = [0]

            def lora(uses):
                for n in uses:
                    m, c = n // KT, n % KT
                    if n >= len(ps_lora):
                        pe.wait_ge(lora_done, n - len(ps_lora) + 1)
                    pe.wait_ge(lora_lo[m // 2], 2)
                    nc.tensor.matmul(ps_lora[n % len(ps_lora)][:], lora_stack[0:STACK, 0, m, c * P:(c + 1) * P],
                                     lora_stack[0:STACK, 1, m, :],
                                     start=True, stop=True).then_inc(lora_ready, 1)

            lora(range(0, 6))
            pe.wait_ge(consts_ready, 3)
            for t in range(TT):
                pe.wait_ge(xn_ready, t + 1)
                transpose_x(t, AT_LN + t, (AT_LN + t) % 2)
            lora(range(6, 10))
            pe.wait_ge(pj_done, AT_LN + TT)
            pe.wait_ge(w_lo_done[0], KT)
            project_q(0, 0, AT_Q[0], AT_Q[0] % 2)
            lora(range(10, 12))
            pe.wait_ge(w_lo_done[1], KT)
            project_q(1, 0, AT_Q[0] + 1, (AT_Q[0] + 1) % 2)
            for m in range(2):
                project_q(m, 1, AT_Q[1] + m, (AT_Q[1] + m) % 2)
            pe.wait_ge(w_lo_done[2], KT)
            for t in range(TT - 1):
                project_v(t, AT_V + t, (AT_V + t) % 2)
            pe.wait_ge(stack_loaded[0], STACK_DMAS)
            for u in range(UNITS):
                maxima_tile(0, u, u)
                if u % 2:
                    m, c = u // (2 * KT), u // 2 % KT
                    project_q(m, 2, AT_Q[2] + m, (AT_Q[2] + m) % 2, range(c, c + 1))
            pe.wait_ge(lora_done, 3 * KT)
            transpose_max(0)
            project_v(TT - 1, PJ_START - 1, (PJ_START - 1) % 2)
            pe.wait_ge(maxT_done, 1)
            lora(range(12, 16))
            pe.wait_ge(lora_done, 4 * KT)
            pe.wait_ge(consts_ready, 3 + GROUPS)

            def body(b, first, last):
                for slot in range(GROUPS):
                    group = GROUPS * b + slot
                    nslot, nb = next_group(slot, b)
                    maxima = not (last and slot == GROUPS - 1)
                    m_next = 0
                    pe.wait_ge(row_loaded, 16 * (group + 1))
                    for u in range(UNITS):
                        kt, j = u // GH, u % GH
                        n = UNITS * group + u
                        if not (first and slot == 0 and u < 2):
                            pe.wait_ge(exp_done, n - 1)
                        s = nc.tensor.matmul(ps_s[u % 2][:], stacks[slot][0:STACK + 1, 1, j, kt * P:(kt + 1) * P],
                                             stacks[slot][0:STACK + 1, 0, j, :], start=True, stop=True)
                        s.then_inc(s_ready, 1)
                        if u in (6, 10, 14):
                            weigh(b, slot, group, (u - 6) // GH)
                        if slot == 1 and not last and u in LN_AFTER:
                            t = LN_AFTER[u]
                            pe.wait_ge(xn_ready, TT * (b + 1) + t + 1)
                            transpose_x(t, *pj(b, "ln", 0, t))
                        if u in PROJECT_AFTER and slot != 1 and (slot == 0 or not last):
                            c = PROJECT_AFTER.index(u)
                            project_q(0, (slot + 3) % GROUPS, *pj(b, "q", slot), range(c, c + 1))
                        if last and slot >= 2 and u in LN2_AFTER:
                            transpose_xn2(slot - 2, LN2_AFTER[u])
                        if last and slot == 3 and u % 2:
                            gate_up(0, 0, 0, 0, range(u // 2, u // 2 + 1))
                        if maxima:
                            for _ in range(M_AFTER[u]):
                                if m_next == 0:
                                    pe.wait_ge(stack_loaded[nslot], STACK_DMAS * (nb + 1))
                                maxima_tile(nslot, m_next, UNITS * (group + 1) + m_next)
                                m_next += 1
                    project = slot == 0 or not last
                    if project:
                        if slot == 1:
                            pe.wait_ge(pj_done, pj(b, "ln", 0, TT - 1)[0] + 1)
                        if slot == 1:
                            project_q(0, 0, *pj(b, "q", slot), range(0, KT // 2))
                        else:
                            project_q(1, (slot + 3) % GROUPS, *pj(b, "k", slot), range(0, K_BEFORE))
                    if maxima:
                        GPAR[0] = (slot + 1) % 2
                        transpose_max(group + 1)
                    weigh(b, slot, group, KK - 1)
                    if maxima:
                        pe.wait_ge(maxT_done, group + 2)
                    else:
                        pe.wait_ge(recip_done, group)
                    pe.wait_ge(psum_added, 2 * GH * (group + 1))
                    for j in range(GH):
                        nc.tensor.matmul(ps_sum[j * HD:(j + 1) * HD, :], ones[:], p_sum[:, j, :], start=True, stop=False)
                        last_mm = nc.tensor.matmul(ps_sum[j * HD:(j + 1) * HD, :], ones[:], probs[:, (KK - 1) % 2, j, :],
                                                   start=False, stop=True)
                    last_mm.then_inc(sum_ready, 1)
                    if project:
                        if slot == 1:
                            project_q(0, 0, *pj(b, "q", slot), range(KT // 2, KT))
                        project_q(1, (slot + 3) % GROUPS, *pj(b, "k", slot), range(0 if slot == 1 else K_BEFORE, KT))
                    if slot == 0 and not last:
                        for t in range(2):
                            pe.wait_ge(xn_ready, TT * (b + 1) + t + 1)
                            transpose_x(t, *pj(b, "ln", 0, t))
                if not last:
                    for t in range(TT):
                        project_v(t, *pj(b, "v", 0, t))
                if first:
                    pe.wait_ge(w_lo_done[3], KT)
                if last:
                    transpose_xn2(2, 0)
                    transpose_xn2(2, 1)
                    gate_up(0, 0, 0, 1)
                    transpose_xn2(2, 2)
                    transpose_xn2(2, 3)
                pe.wait_ge(oT_lo_done, GROUPS * (b + 1))
                for t in range(TT):
                    o_use, bank = pj(b, "o", 0, t)
                    pj_free(o_use)
                    for g in range(GROUPS):
                        last_mm = three(ps_pj[bank][:], oT_hi[:, g, t * P:(t + 1) * P], oT_lo[:, g, t * P:(t + 1) * P],
                                        w_hi[3][:, g, :], w_lo[3][:, g, :], g == 0, g == GROUPS - 1)
                    last_mm.then_inc(pj_ready, 1)

            def weigh(b, slot, group, kt):
                pe.wait_ge(exp_done, UNITS * group + GH * (kt + 1))
                if kt == 0:
                    if not isinstance(group, int) or group >= 1:
                        pe.wait_ge(o_raw_done, group)
                    if slot == 0:
                        v_at = PJ_START - 1 if isinstance(b, int) and b == 0 else pj(b - 1, "v", 0, TT - 1)[0]
                        pe.wait_ge(pj_done, v_at + 1)
                for j in range(GH):
                    head = slot * GH + j
                    mm = nc.tensor.matmul(ps_o[j * HD:(j + 1) * HD, :], v_sb[:, kt, head * HD:(head + 1) * HD],
                                          probs[:, kt % 2, j, :], start=kt == 0, stop=kt == KK - 1)
                mm.then_inc(pv_done, 1)

            def transpose_xn2(c, t):
                pe.wait_ge(xn2_ready, TT * c + t + 1)
                use, bank = pj(LAST, "ln2", c, t)
                pj_free(use)
                for k in range(KT):
                    mm = nc.tensor.transpose(ps_pj[bank][:, k * P:(k + 1) * P], xn2[c][:, t, k * P:(k + 1) * P], ident[:])
                mm.then_inc(pj_ready, 1)

            def gate_up(q, s, c, j, steps=range(2 * KT)):
                n = J * q + j
                for i in steps:
                    part, k = i // KT, i % KT
                    dst, freed, ready = ((ps_gate, silu_done, gate_ready), (ps_up, h_ready, up_ready))[part]
                    if i == 0 and c == 0:
                        pe.wait_ge(ffw_lo, 5 * s + j + 1)
                    if i == 0 and isinstance(q, int) and q < BATCHES and j == 0:
                        pe.wait_ge(pj_done, pj(LAST, "ln2", c, TT - 1)[0] + 1)
                    if k == 0 and (not isinstance(n, int) or n >= 2):
                        pe.wait_ge(freed, n - 1)
                    mm = three(dst[j % 2][:], gu_hi[:, j, part, k * P:(k + 1) * P], gu_lo[:, j, part, k * P:(k + 1) * P],
                               xn2T_hi[c][:, k, :], xn2T_lo[c][:, k, :], k == 0, k == KT - 1)
                    if k == KT - 1:
                        mm.then_inc(ready, 1)

            per_batch(body, pe, pe.Fori)

            def down(q, s, c):
                if c == 0:
                    pe.wait_ge(ffw_lo, 5 * s + 5)
                pe.wait_ge(hT_lo_done, q + 1)
                pe.wait_ge(hT_hi_done, q + 1)
                for t in range(TT):
                    if not isinstance(q, int) or q >= 1:
                        pe.wait_ge(y_done, TT * (q - 1) + t + 1)
                    for j in range(J):
                        mm = three(ps_y[t][:], hT_hi[:, j, t * P:(t + 1) * P], hT_lo[:, j, t * P:(t + 1) * P],
                                   dn_hi[:, j, :], dn_lo[:, j, :], j == 0, j == J - 1)
                    mm.then_inc(down_ready, 1)

            def block_step(s, first, last):
                for c in range(BATCHES):
                    q = BATCHES * s + c
                    for j in range(2 if first and c == 0 else 0, J):
                        gate_up(q, s, c, j)
                    if first and c == 1:
                        for t in range(TT):
                            transpose_xn2(LAST, t)
                        pe.wait_ge(pj_done, pj(LAST, "ln2", LAST, TT - 1)[0] + 1)
                    if c:
                        down(q - 1, s, c - 1)
                    elif not first:
                        down(q - 1, s - 1, BATCHES - 1)

            per_block(block_step, pe.Fori)
            down(NT - 1, SB - 1, BATCHES - 1)

        @block.gpsimd
        def _(pool):
            nc.gpsimd.memset(ident[:], 0.0).then_inc(ident_zeroed, 1)
            nc.gpsimd.memset(lora_raw[0:STACK, 1], 0.0).then_inc(lora_zeroed[1], 1)
            pool.wait_ge(lora_zeroed[1], 1)
            nc.gpsimd.memset(neg_half[:], -0.5).then_inc(consts_ready, 1)
            nc.gpsimd.memset(ones[:], 1.0).then_inc(consts_ready, 1)
            pool.wait_ge(ident_zeroed, 1)
            nc.gpsimd.affine_select(out=ident[:], in_=ident[:], compare_op=ALU.not_equal, fill=1.0, base=0,
                                    pattern=[[-1, P]], channel_multiplier=1).then_inc(consts_ready, 1)

            def inverse_deviation(n, at):
                pool.wait_ge(var_ready, n + 1)
                nc.gpsimd.tensor_tensor(rstd[:, at], var_eps[:, at], neg_half[:, at], ALU.pow).then_inc(rstd_ready, 1)

            def weight_lo(m):
                for c in range(KT):
                    pool.wait_ge(w_hi_done[m], c + 1)
                    nc.gpsimd.tensor_tensor(w_lo[m][:, c], w_raw[m][:, c], w_hi[m][:, c].bitcast(F32), ALU.subtract)\
                      .then_inc(w_lo_done[m], 1)

            pool.wait_ge(consts_ready, 3)
            inverse_deviation(0, slice(0, TT))
            weight_lo(0)
            weight_lo(2)
            pool.wait_ge(w_lo_done[2], KT)
            for g in range(GROUPS):
                pool.wait_ge(consts_ready, 3 + g)
                nc.gpsimd.memset(stacks[g][STACK:STACK + 1, 1, :, :].bitcast(F32), 1.0).then_inc(consts_ready, 1)
            pool.wait_ge(consts_ready, 3 + GROUPS)
            weight_lo(3)

            def body(b, first, last):
                for slot in range(GROUPS):
                    group = GROUPS * b + slot
                    for kt in range(1, KK - 1):
                        if slot < 2 and not last and kt == 2:
                            inverse_deviation(2 * b + slot + 1, slice(2 * slot, 2 * slot + 2))
                        if last and slot >= 2 and kt == 2:
                            for pair in range(2):
                                inverse_deviation2(2 * (slot - 2) + pair)
                        for j in range(GH):
                            pool.wait_ge(exp_done, UNITS * group + GH * kt + j + 1)
                            if kt == 1:
                                if not isinstance(group, int) or group >= 1:
                                    pool.wait_ge(sum_ready, group)
                                a = probs[:, 0, j, :]
                            else:
                                pool.wait_ge(psum_added, 2 * GH * group + GH * (kt - 2) + j + 1)
                                a = p_sum[:, j, :]
                            nc.gpsimd.tensor_tensor(p_sum[:, j, :], a, probs[:, kt % 2, j, :], ALU.add).then_inc(psum_added, 1)
                    if last and slot == 1:
                        add_bias(b, first)
                    if last and slot == 2:
                        for j in range(J):
                            split_gu(0, j)
                if not last:
                    add_bias(b, first)

            def add_bias(b, first):
                if first:
                    pool.wait_ge(bo_loaded, 16)
                pool.wait_ge(x_res_loaded, 16 * (b + 1))
                for t in range(TT):
                    nc.gpsimd.tensor_tensor(x_res[:, t, :], x_res[:, t, :], bo_sb[:], ALU.add).then_inc(x_res_ready, 1)

            def inverse_deviation2(pair):
                pool.wait_ge(var2_ready, pair + 1)
                at = slice(pair % 2 * 2, pair % 2 * 2 + 2)
                nc.gpsimd.tensor_tensor(rstd[:, at], var_eps[:, at], neg_half[:, at], ALU.pow).then_inc(rstd2_ready, 1)

            def split_gu(s, j):
                pool.wait_ge(ffw_hi, 5 * s + j + 1)
                nc.gpsimd.tensor_tensor(gu_lo[:, j], gu_raw[:, j], gu_hi[:, j].bitcast(F32), ALU.subtract).then_inc(ffw_lo, 1)

            def split_dn(s):
                pool.wait_ge(ffw_hi, 5 * s + 5)
                nc.gpsimd.tensor_tensor(dn_lo[:], dn_raw[:], dn_hi[:].bitcast(F32), ALU.subtract).then_inc(ffw_lo, 1)

            per_batch(body, pool, pool.Fori)

            for pair in range(4, 6):
                inverse_deviation2(pair)
            split_dn(0)
            for pair in range(6, 8):
                inverse_deviation2(pair)

            def block_step(s, first, last):
                if not first:
                    split_dn(s)
                if not last:
                    for j in range(J):
                        split_gu(s + 1, j)

            per_block(block_step, pool.Fori)

        @block.scalar
        def _(act):
            def hi_of(dst, src, bias_col=None):
                if bias_col is None:
                    return nc.scalar.activation(dst, src, ACT.Copy)
                return nc.scalar.activation(dst, src, ACT.Identity, bias=bias_col)

            def xnT_part(t, use, bank):
                act.wait_ge(pj_ready, use + 1)
                hi_of(xnT_hi[:, :, t * P:(t + 1) * P],
                      ps_pj[bank][:].rearrange("p (c n) -> p c n", c=KT)).then_inc(xnT_hi_done, 1)

            def qk_part(m, g, use, bank, parts=qk_parts):
                act.wait_ge(pj_ready, use + 1)
                hi_of(parts[:, (Q_HI, K_HI)[m], :], ps_pj[bank][:], bias[:, m, g:g + 1]).then_inc(qk_hi_done, 1)

            def max_row(slot, group):
                act.wait_ge(maxT_ready, group + 1)
                if not isinstance(group, int) or group >= 1:
                    act.wait_ge(row_loaded, 16 * group)
                hi_of(row_max[0:UNITS, :], ps_sum[0:UNITS, 0:P]).then_inc(maxT_done, 1)
                act.wait_ge(maxT_done, group + 1)
                act.dma_start(stacks[slot][STACK:STACK + 1, 0, :, :].bitcast(F32), row_max[0:UNITS, :].bitcast(F32))\
                   .then_inc(row_loaded, 16)

            def weight_hi(m):
                for c in range(KT):
                    act.wait_ge(lora_done, KT * m + c + 1)
                    hi_of(w_hi[m][:, c], w_raw[m][:, c]).then_inc(w_hi_done[m], 1)

            act.wait_ge(lora_loaded, 16 * 6)
            for half in range(2):
                for side in range(2):
                    hi_of(lora_stack[0:STACK, side, 2 * half:2 * half + 2], lora_raw[0:STACK, side, 2 * half:2 * half + 2]).then_inc(lora_hi, 1)
            weight_hi(0)
            for t in range(TT):
                xnT_part(t, AT_LN + t, (AT_LN + t) % 2)
            weight_hi(1)
            act.wait_ge(bias_loaded, 16)
            weight_hi(2)
            qk_part(0, 0, AT_Q[0], AT_Q[0] % 2)
            qk_part(1, 0, AT_Q[0] + 1, (AT_Q[0] + 1) % 2)
            qk_part(0, 1, AT_Q[1], AT_Q[1] % 2, qk_parts1)
            qk_part(1, 1, AT_Q[1] + 1, (AT_Q[1] + 1) % 2, qk_parts1)
            act.wait_ge(stack_loaded[0], STACK_DMAS)
            qk_part(0, 2, AT_Q[2], AT_Q[2] % 2)
            qk_part(1, 2, AT_Q[2] + 1, (AT_Q[2] + 1) % 2)
            max_row(0, 0)
            weight_hi(3)

            def body(b, first, last):
                for slot in range(GROUPS):
                    group = GROUPS * b + slot
                    nslot, nb = next_group(slot, b)
                    maxima = not (last and slot == GROUPS - 1)
                    for u in range(UNITS):
                        kt, j = u // GH, u % GH
                        n = UNITS * group + u
                        act.wait_ge(s_ready, n + 1)
                        if not (first and slot == 0 and kt < 2):
                            if j == 0:
                                act.wait_ge(pv_done, KK * group + kt - 1)
                            if kt == 1:
                                if j == 0:
                                    act.wait_ge(sum_ready, group)
                            else:
                                act.wait_ge(psum_added, 2 * GH * group + (j + 1 if kt else j + 1 - GH))
                        nc.scalar.activation(probs[:, kt % 2, j, :], ps_s[u % 2][:], ACT.Exp, scale=SCALE).then_inc(exp_done, 1)
                        if slot == 1 and not last and u in LN_AFTER:
                            xnT_part(LN_AFTER[u], *pj(b, "ln", 0, LN_AFTER[u]))
                        if last and slot >= 2 and u in LN2_AFTER:
                            xn2T_part(slot - 2, LN2_AFTER[u])
                        if last and slot == 2 and u % 4 == 3:
                            gu_hi_part(0, u // 4)
                    project = slot == 0 or not last
                    if project and slot != 1:
                        stack_free(b, slot)
                        qk_part(0, (slot + 3) % GROUPS, *pj(b, "q", slot))
                    if maxima:
                        max_row(nslot, group + 1)
                    if project:
                        if slot == 1:
                            stack_free(b, slot)
                            qk_part(0, 0, *pj(b, "q", slot))
                        qk_part(1, (slot + 3) % GROUPS, *pj(b, "k", slot))
                    if slot == 0 and not last:
                        for t in range(2):
                            xnT_part(t, *pj(b, "ln", 0, t))
                if last:
                    act.wait_ge(sum_ready, GROUPS * BATCHES)
                    gate(0, 0)
                    xn2T_part(2, 0)
                    xn2T_part(2, 1)
                    dn_hi_part(0)
                act.wait_ge(o_raw_done, GROUPS * (b + 1))
                for g in range(GROUPS):
                    hi_of(oT_hi[:, g, :], o_raw[:, g, :], bias[:, 2, g:g + 1]).then_inc(oT_hi_done, 1)

            def gu_hi_part(s, j):
                act.wait_ge(gu_loaded[j], 16 * (s + 1))
                hi_of(gu_hi[:, j], gu_raw[:, j]).then_inc(ffw_hi, 1)

            def dn_hi_part(s):
                act.wait_ge(dn_loaded, 16 * (s + 1))
                hi_of(dn_hi[:], dn_raw[:]).then_inc(ffw_hi, 1)

            def xn2T_part(c, t):
                use, bank = pj(LAST, "ln2", c, t)
                act.wait_ge(pj_ready, use + 1)
                hi_of(xn2T_hi[c][:, :, t * P:(t + 1) * P],
                      ps_pj[bank][:].rearrange("p (c n) -> p c n", c=KT)).then_inc(xn2T_hi_done, 1)

            def gate(q, j):
                n = J * q + j
                act.wait_ge(gate_ready, n + 1)
                if not isinstance(n, int) or n >= 2:
                    act.wait_ge(h_ready, n - 1)
                nc.scalar.activation(silu[:, j % 2, :], ps_gate[j % 2][:], ACT.Silu).then_inc(silu_done, 1)

            def stack_free(b, slot):
                act.wait_ge(stack_loaded[(slot + 2) % GROUPS], STACK_DMAS * (b + (1 if slot < 2 else 2)))

            per_batch(body, act, act.Fori)

            gate(0, 1)
            xn2T_part(2, 2)
            xn2T_part(2, 3)
            act.wait_ge(pj_ready, pj(LAST, "o", 0, TT - 1)[0] + 1)

            def block_step(s, first, last):
                for c in range(BATCHES):
                    q = BATCHES * s + c

                    def size(j):
                        act.wait_ge(h_ready, J * q + j + 1)
                        if not first or c >= 1:
                            act.wait_ge(mask_step, 10 * (q - 1) + 3)
                        nc.scalar.activation(h_abs[:, j, :], h[:, j, :], ACT.Abs).then_inc(abs_done, 1)

                    if not first or c:
                        gate(q, 0)
                        gate(q, 1)
                    if c == 1 and not first:
                        dn_hi_part(s)
                    size(0)
                    gate(q, 2)
                    size(1)
                    gate(q, 3)
                    if first and c == 1:
                        for t in range(TT):
                            xn2T_part(LAST, t)
                    size(2)
                    if c == BATCHES - 1 and not last:
                        gu_hi_part(s + 1, 0)
                        gu_hi_part(s + 1, 1)
                    size(3)
                    if c == BATCHES - 1 and not last:
                        gu_hi_part(s + 1, 2)
                        gu_hi_part(s + 1, 3)
                    if not first or c >= 1:
                        act.wait_ge(down_ready, TT * q)
                    act.wait_ge(h_kept, J * (q + 1))
                    hi_of(hT_hi[:], h[:]).then_inc(hT_hi_done, 1)

            per_block(block_step, act.Fori)

        @block.vector
        def _(dve):
            def statistics(src, step, var_sem, loaded, count, tiles=range(TT), arrived=16):
                n = len(tiles)
                dve.wait_ge(loaded, arrived)
                for t in tiles:
                    nc.vector.bn_stats(stats[:, t, :], src(t)).then_inc(step, 1)
                for i, t in enumerate(tiles):
                    dve.wait_ge(step, count + i + 1)
                    nc.vector.bn_aggr(mv[:, t, :], stats[:, t, :]).then_inc(step, 1)
                dve.wait_ge(step, count + 2 * n)
                at = slice(tiles[0], tiles[0] + n)
                nc.vector.tensor_scalar(var_eps[:, at], mv[:, at, 1], EPS, None, ALU.add).then_inc(var_sem, 1)

            def normalise(dst, src, mean, r):
                return nc.vector.tensor_scalar(dst, src, mean, r, ALU.subtract, ALU.mult)

            def xnT_part(t, use, bank, n):
                dve.wait_ge(xnT_hi_done, n + 1)
                nc.vector.tensor_tensor(xnT_lo[:, :, t * P:(t + 1) * P],
                                        ps_pj[bank][:].rearrange("p (c n) -> p c n", c=KT),
                                        xnT_hi[:, :, t * P:(t + 1) * P].bitcast(F32), ALU.subtract).then_inc(pj_done, 1)

            def qk_part(m, g, bank, n, parts=qk_parts):
                dve.wait_ge(qk_hi_done, n + 1)
                nc.vector.scalar_tensor_tensor(parts[:, (Q_LO, K_LO)[m], :], ps_pj[bank][:], bias[:, m, g:g + 1],
                                               parts[:, (Q_HI, K_HI)[m], :].bitcast(F32), ALU.add, ALU.subtract).then_inc(pj_done, 1)

            def v_part(t, use, bank):
                dve.wait_ge(pj_ready, use + 1)
                nc.vector.tensor_copy(v_sb[:, t, :], ps_pj[bank][:]).then_inc(pj_done, 1)

            def reduce(u, n, par):
                dve.wait_ge(m_ready, n + 1)
                nc.vector.tensor_reduce(neg_max[:, par, u:u + 1], ps_m[u % 2][:], AX.X, ALU.max, negate=True).then_inc(m_done, 1)

            def lora_part(m):
                dve.wait_ge(w_loaded[m], 16)
                for c in range(KT):
                    n = KT * m + c
                    dve.wait_ge(lora_ready, n + 1)
                    nc.vector.scalar_tensor_tensor(w_raw[m][:, c, :], ps_lora[n % len(ps_lora)][:], LORA, w_raw[m][:, c, :],
                                                   ALU.mult, ALU.add).then_inc(lora_done, 1)

            nc.vector.memset(lora_raw[0:STACK, 0], 0.0).then_inc(lora_zeroed[0], 1)
            statistics(lambda t: x_first[:, t, :], stats_step, var_ready, x_first_loaded, 0)
            split_lora_lo(dve, nc.vector, 0)
            dve.wait_ge(rstd_ready, 1)
            for t in range(2):
                normalise(x_in[:, t, :], x_first[:, t, :], mv[:, t, 0:1], rstd[:, t:t + 1]).then_inc(xn_ready, 1)
            lora_part(0)
            split_lora_lo(dve, nc.vector, 1)
            for t in range(TT):
                xnT_part(t, AT_LN + t, (AT_LN + t) % 2, t)
                if t < 2:
                    normalise(x_in[:, t, :], x_first[:, t + 2, :], mv[:, t + 2, 0:1], rstd[:, t + 2:t + 3]).then_inc(xn_ready, 1)
            lora_part(1)
            for c in range(KT):
                dve.wait_ge(w_hi_done[1], c + 1)
                nc.vector.tensor_tensor(w_lo[1][:, c], w_raw[1][:, c], w_hi[1][:, c].bitcast(F32), ALU.subtract)\
                  .then_inc(w_lo_done[1], 1)
            dve.wait_ge(bias_loaded, 16)
            lora_part(2)
            qk_part(0, 0, AT_Q[0] % 2, 0)
            qk_part(1, 0, (AT_Q[0] + 1) % 2, 1)
            qk_part(0, 1, AT_Q[1] % 2, 2, qk_parts1)
            qk_part(1, 1, (AT_Q[1] + 1) % 2, 3, qk_parts1)
            for t in range(TT - 1):
                v_part(t, AT_V + t, (AT_V + t) % 2)
            for u in range(UNITS):
                reduce(u, u, 0)
                if u == 9:
                    qk_part(0, 2, AT_Q[2] % 2, 4)
            qk_part(1, 2, (AT_Q[2] + 1) % 2, 5)
            v_part(TT - 1, PJ_START - 1, (PJ_START - 1) % 2)
            lora_part(3)

            def body(b, first, last):
                for slot in range(GROUPS):
                    group = GROUPS * b + slot
                    maxima = not (last and slot == GROUPS - 1)
                    m_next = 0
                    for u in range(UNITS):
                        if slot == 1 and not last and u in LN_AFTER:
                            t = LN_AFTER[u]
                            ln_use, bank = pj(b, "ln", 0, t)
                            xnT_part(t, ln_use, bank, TT * (b + 1) + t)
                        step = LN_STEPS[slot].get(u) if slot < 2 and not last else None
                        if step in (2, 3):
                            dve.wait_ge(stats_step, 2 * TT * (b + 1) + TT * slot + 2 * (step - 1))
                        if maxima:
                            for _ in range(M_AFTER[u]):
                                reduce(m_next, UNITS * (group + 1) + m_next, (slot + 1) % 2)
                                m_next += 1
                        if step is not None:
                            next_tiles(b, slot, step)
                        if last and slot >= 2:
                            if u in STATS2_AFTER:
                                statistics2(slot - 2, STATS2_AFTER[u])
                            if u in NORMALISE2_AFTER:
                                normalise2(slot - 2, NORMALISE2_AFTER[u])
                            if u in LN2_AFTER:
                                xn2T_part(slot - 2, LN2_AFTER[u])
                    if last and slot == GROUPS - 1:
                        for pair in range(2):
                            statistics2(2, pair)
                        dve.wait_ge(s_ready, UNITS * GROUPS * BATCHES)
                        for pair in range(2):
                            normalise2(2, pair)
                    project = slot == 0 or not last
                    if project and slot != 1:
                        qk_part(0, (slot + 3) % GROUPS, pj(b, "q", slot)[1], 6 + 8 * b + 2 * slot)
                    dve.wait_ge(sum_ready, group + 1)
                    nc.vector.reciprocal(recip[:], ps_sum[:]).then_inc(recip_done, 1)
                    dve.wait_ge(recip_done, group + 1)
                    if slot == 0 and not first:
                        dve.wait_ge(oT_hi_done, GROUPS * b)
                    nc.vector.tensor_tensor(o_raw[:, slot, :], ps_o[:], recip[:], ALU.mult).then_inc(o_raw_done, 1)
                    if project:
                        for m, what in enumerate("qk"):
                            if m or slot == 1:
                                qk_part(m, (slot + 3) % GROUPS, pj(b, what, slot)[1], 6 + 8 * b + 2 * slot + m)
                    if slot == 0 and not last:
                        for t in range(2):
                            xnT_part(t, *pj(b, "ln", 0, t), TT * (b + 1) + t)
                if last:
                    xn2T_part(2, 0)
                    xn2T_part(2, 1)
                for g in range(GROUPS):
                    if not last and g < 3:
                        v_part(g, *pj(b, "v", 0, g))
                    dve.wait_ge(oT_hi_done, GROUPS * b + g + 1)
                    nc.vector.scalar_tensor_tensor(oT_lo[:, g, :], o_raw[:, g, :], bias[:, 2, g:g + 1],
                                                   oT_hi[:, g, :].bitcast(F32), ALU.add, ALU.subtract).then_inc(oT_lo_done, 1)
                if not last:
                    v_part(3, *pj(b, "v", 0, 3))
                if last:
                    dve.wait_ge(oT_lo_done, GROUPS * BATCHES)
                    dve.wait_ge(x_res_ready, NT)
                    xn2T_part(2, 2)
                    xn2T_part(2, 3)
                    product(0, 0)
                    product(0, 1)
                for t in range(TT):
                    o_use, bank = pj(b, "o", 0, t)
                    dve.wait_ge(pj_ready, o_use + 1)
                    dve.wait_ge(x_res_ready, TT * b + t + 1)
                    nc.vector.tensor_tensor(x_res[:, t, :], ps_pj[bank][:], x_res[:, t, :], ALU.add).then_inc(pj_done, 1)

            def next_tiles(b, pair, step):
                tiles = slice(2 * pair, 2 * pair + 2)
                if step < 2:
                    dve.wait_ge(x_in_loaded[step], 32 * b + 16 * (pair + 1))
                    nc.vector.bn_stats(stats[:, 2 * pair + step, :], x_in[:, step, :]).then_inc(stats_step, 1)
                elif step == 2:
                    for t in range(2 * pair, 2 * pair + 2):
                        nc.vector.bn_aggr(mv[:, t, :], stats[:, t, :]).then_inc(stats_step, 1)
                elif step == 3:
                    nc.vector.tensor_scalar(var_eps[:, tiles], mv[:, tiles, 1], EPS, None, ALU.add).then_inc(var_ready, 1)
                else:
                    t = 2 * pair + step - 4
                    dve.wait_ge(rstd_ready, 2 * b + pair + 2)
                    normalise(x_in[:, t % 2, :], x_in[:, t % 2, :], mv[:, t, 0:1], rstd[:, t:t + 1]).then_inc(xn_ready, 1)

            def statistics2(c, pair):
                n = 2 * c + pair
                if c < LAST:
                    dve.wait_ge(x2_back[c], 16)
                else:
                    dve.wait_ge(pj_done, pj(LAST, "o", 0, TT - 1)[0] + 1)
                if pair == 0 and c:
                    dve.wait_ge(rstd2_ready, 2 * c)
                statistics(lambda t: y[:, c * TT + t, :], stats2_step, var2_ready, stats2_step, 4 * n,
                           range(2 * pair, 2 * pair + 2), 4 * n)

            def normalise2(c, pair):
                dve.wait_ge(rstd2_ready, 2 * c + pair + 1)
                for t in range(2 * pair, 2 * pair + 2):
                    normalise(xn2[c][:, t, :], y[:, c * TT + t, :], mv[:, t, 0:1], rstd[:, t:t + 1]).then_inc(xn2_ready, 1)

            def xn2T_part(c, t):
                dve.wait_ge(xn2T_hi_done, TT * c + t + 1)
                bank = pj(LAST, "ln2", c, t)[1]
                at = slice(t * P, (t + 1) * P)
                nc.vector.tensor_tensor(xn2T_lo[c][:, :, at], ps_pj[bank][:].rearrange("p (c n) -> p c n", c=KT),
                                        xn2T_hi[c][:, :, at].bitcast(F32), ALU.subtract).then_inc(pj_done, 1)

            def product(q, j):
                n = J * q + j
                dve.wait_ge(up_ready, n + 1)
                dve.wait_ge(silu_done, n + 1)
                if j == 0 and not (isinstance(q, int) and q == 0):
                    dve.wait_ge(hT_hi_done, q)
                    dve.wait_ge(hT_lo_done, q)
                nc.vector.tensor_tensor(h[:, j, :], ps_up[j % 2][:], silu[:, j % 2, :], ALU.mult).then_inc(h_ready, 1)

            per_batch(body, dve, dve.Fori)

            def add_down(q, c):
                for t in range(TT):
                    dve.wait_ge(down_ready, TT * q + t + 1)
                    nc.vector.tensor_tensor(y[:, c * TT + t, :], ps_y[t][:], y[:, c * TT + t, :], ALU.add).then_inc(y_done, 1)

            def block_step(s, first, last):
                for c in range(BATCHES):
                    q = BATCHES * s + c
                    for j in range(2 if first and c == 0 else 0, J):
                        product(q, j)
                        if first and c == 1:
                            if j < 2:
                                statistics2(LAST, j)
                            if j == 2:
                                for pair in range(2):
                                    normalise2(LAST, pair)
                            if j == 3:
                                for t in range(TT):
                                    xn2T_part(LAST, t)
                    step = 10 * q
                    dve.wait_ge(abs_done, J * (q + 1))
                    nc.vector.tensor_tensor(pair_max[:], h_abs[:, 0:J:2, :], h_abs[:, 1:J:2, :], ALU.max).then_inc(mask_step, 1)
                    nc.vector.tensor_tensor(pair_min[:], h_abs[:, 0:J:2, :], h_abs[:, 1:J:2, :], ALU.min).then_inc(mask_step, 1)
                    nc.vector.tensor_tensor(first_wins[:], h_abs[:, 0:J:2, :], h_abs[:, 1:J:2, :], ALU.is_ge).then_inc(mask_step, 1)
                    dve.wait_ge(mask_step, step + 2)
                    nc.vector.tensor_tensor(both_01[:], pair_min[:, 0, :], pair_max[:, 1, :], ALU.is_ge).then_inc(mask_step, 1)
                    nc.vector.tensor_tensor(both_23[:], pair_min[:, 1, :], pair_max[:, 0, :], ALU.is_gt).then_inc(mask_step, 1)
                    dve.wait_ge(mask_step, step + 5)
                    nc.vector.tensor_tensor(tilt[:], both_01[:], both_23[:], ALU.subtract).then_inc(mask_step, 1)
                    dve.wait_ge(mask_step, step + 6)
                    for i in range(2):
                        nc.vector.tensor_tensor(wins_up[:, i, :], first_wins[:, i, :], tilt[:], ALU.add).then_inc(mask_step, 1)
                        nc.vector.tensor_tensor(wins_down[:, i, :], first_wins[:, i, :], tilt[:], ALU.subtract).then_inc(mask_step, 1)
                    dve.wait_ge(mask_step, step + 10)
                    kept = ((wins_up, 0, ALU.is_ge, 1.0), (wins_down, 0, ALU.is_le, 0.0),
                            (wins_down, 1, ALU.is_ge, 1.0), (wins_up, 1, ALU.is_le, 0.0))
                    for j, (wins, i, op, bound) in enumerate(kept):
                        nc.vector.scalar_tensor_tensor(h[:, j, :], wins[:, i, :], bound, h[:, j, :], op, ALU.mult).then_inc(h_kept, 1)
                    dve.wait_ge(hT_hi_done, q + 1)
                    nc.vector.tensor_tensor(hT_lo[:], h[:], hT_hi[:].bitcast(F32), ALU.subtract).then_inc(hT_lo_done, 1)
                    if c:
                        add_down(q - 1, c - 1)
                    elif not first:
                        add_down(q - 1, BATCHES - 1)

            per_block(block_step, dve.Fori)
            add_down(NT - 1, BATCHES - 1)


def kernel(**inputs):
    import numpy as np
    import concourse.bacc as bacc
    from concourse.bass_utils import run_bass_kernel_spmd

    a = {k.replace("L0_attn_", "").replace("L0_ffn_", ""): np.asarray(v) for k, v in inputs.items()}
    names = "qkvo"
    arrays = {
        "x_in": a["x"].reshape(NT, P, D).transpose(1, 0, 2),
        "wqkvo_in": np.stack([a["W" + n].T.reshape(KT, P, D).transpose(1, 0, 2) for n in names]),
        "lora_b_in": np.stack([a["B" + n] for n in names], axis=1),
        "lora_a_in": np.stack([a["A" + n].T for n in names], axis=1),
        "bias_cols_in": np.stack([a["b" + n].reshape(KT, P).T for n in "qkv"], axis=1),
        "bo_rows_in": np.broadcast_to(a["bo"], (P, D)),
        "w_gu_in": np.stack([a["w_" + n].reshape(KT, P, SB, P, J).transpose(1, 2, 4, 0, 3) for n in ("gate", "up")], axis=3)
                     .reshape(P, SB, J, 2, KT * P),
        "w_down_in": a["w_down"].reshape(SB, P, J, D).transpose(1, 0, 2, 3),
    }
    arrays = {k: np.ascontiguousarray(v) for k, v in arrays.items()}
    nc = bacc.Bacc("TRN2", target_bir_lowering=False, num_devices=1)
    args = [nc.dram_tensor(k, v.shape, mybir.dt.from_np(v.dtype), kind="ExternalInput").ap() for k, v in arrays.items()]
    out = nc.dram_tensor("x_out", (P, NT, D), F32, kind="ExternalOutput").ap()
    block_kernel(nc, *args, out)
    r = run_bass_kernel_spmd(nc, [arrays], core_ids=[0])
    got = r.results[0]["x_out"]
    return np.ascontiguousarray(got.transpose(1, 0, 2)).reshape(BATCHES, L, D)
```
